# Optimizing a Trainium2 kernel written in Bass

```python
import numpy as np
import jax
import jax.numpy as jnp

def _softmax(x, axis=-1):
    return jax.nn.softmax(x, axis=axis)

def _gelu(x):
    return jax.nn.gelu(x, approximate=True)

def _silu(x):
    return jax.nn.silu(x)

def _sigmoid(x):
    return jax.nn.sigmoid(x)

def _layernorm(x, axis=-1, eps=1e-05):
    m = jnp.mean(x, axis=axis, keepdims=True)
    v = jnp.var(x, axis=axis, keepdims=True)
    return (x - m) / jnp.sqrt(v + eps)

def _scatter_add(tgt, idx, src, axis=0):
    return tgt.at[idx].add(src)

def _segment_sum(src, seg, n):
    return jax.ops.segment_sum(src, seg, n)
kernel_name = 'mk_adj_ffn_d2_adj_r2_ed9d74'

def setup_inputs(seed: int=0):
    np.random.seed(seed)
    _w = jnp.asarray

    def _rec_inputs():
        import jax
        import jax.numpy as jnp
        _gk = jax.random.key(seed)
        x = -0.0002928 + 1 * jax.random.normal(jax.random.fold_in(_gk, 1), (16, 512, 128), jnp.float32)
        _a = jax.random.bernoulli(jax.random.fold_in(_gk, 2), 0.03125, (16, 512, 512))
        _a = jnp.logical_or(_a, jnp.swapaxes(_a, -1, -2))
        _a = jnp.logical_or(_a, jnp.eye(512, dtype=bool))
        _af = _a.astype(jnp.float32)
        _af = _af * jax.random.uniform(jax.random.fold_in(_gk, 3), (16, 512, 512), jnp.float32, 0.05, 1)
        adj = _af
        return (x, adj)
    x, adj = _rec_inputs()

    def _L0_gnn_setup():
        import jax, jax.numpy as jnp
        import numpy as np
        B, N, F_IN, F_OUT = (8, 1024, 128, 128)
        key = jax.random.key(seed)
        k1, k2, k3, k4 = jax.random.split(key, 4)
        node_features = jax.random.normal(k1, (B, N, F_IN), dtype=jnp.float32)
        adj_matrix = jax.random.uniform(k2, (B, N, N), dtype=jnp.float32)
        lim = 1.0 / np.sqrt(F_IN)
        W = jax.random.uniform(k3, (F_OUT, F_IN), minval=-lim, maxval=lim, dtype=jnp.float32)
        b = jax.random.uniform(k4, (F_OUT,), minval=-lim, maxval=lim, dtype=jnp.float32)
        return {'node_features': node_features, 'adj_matrix': adj_matrix, 'W': W, 'b': b}
    _L0_gnn_all = _L0_gnn_setup()
    _L0_gnn_in = {k: v for k, v in _L0_gnn_all.items() if k in ('W', 'b')}
    del _L0_gnn_all

    def _L0_ffn_setup():
        import jax, jax.numpy as jnp
        import numpy as np
        IN_CH = 128
        OUT_CH = 128
        key = jax.random.key(seed)
        kx, kw, kb = jax.random.split(key, 3)
        x = jax.random.normal(kx, (8, 2048, IN_CH), dtype=jnp.float32)
        bound = 1.0 / np.sqrt(IN_CH)
        weight = jax.random.uniform(kw, (OUT_CH, IN_CH), dtype=jnp.float32, minval=-bound, maxval=bound)
        bias = jax.random.uniform(kb, (OUT_CH,), dtype=jnp.float32, minval=-bound, maxval=bound)
        return {'x': x, 'weight': weight, 'bias': bias}
    _L0_ffn_all = _L0_ffn_setup()
    _L0_ffn_in = {k: v for k, v in _L0_ffn_all.items() if k in ('weight', 'bias')}
    del _L0_ffn_all

    def _L1_gnn_setup():
        import jax, jax.numpy as jnp
        import numpy as np
        from jax import lax
        DIM = 128
        EPS = 1e-05

        def _bn(h, g, b, m, v):
            scale = g / jnp.sqrt(v + EPS)
            return h * scale[None, :, None] + (b - m * scale)[None, :, None]

        def _conv1d(h, w, pad):
            return lax.conv_general_dilated(h, w, window_strides=(1,), padding=[(pad, pad)], dimension_numbers=('NCH', 'OIH', 'NCH'))
        key = jax.random.key(seed)
        ks = jax.random.split(key, 16)
        bs, n, d = (16, 1024, DIM)
        s = 0.05
        return {'x': jax.random.normal(ks[0], (bs, n, d), jnp.float32), 'mask': jnp.ones((bs, n, n), jnp.float32), 'w_se': jax.random.normal(ks[1], (3, d), jnp.float32) * s, 'b_se': jnp.zeros((3,), jnp.float32), 'conv1_w': jax.random.normal(ks[2], (d, d, 1), jnp.float32) * s, 'bn1_g': jnp.ones((d,), jnp.float32), 'bn1_b': jnp.zeros((d,), jnp.float32), 'bn1_m': jnp.zeros((d,), jnp.float32), 'bn1_v': jnp.ones((d,), jnp.float32), 'conv2_w': jax.random.normal(ks[3], (d, d, 17), jnp.float32) * s, 'bn2_g': jnp.ones((d,), jnp.float32), 'bn2_b': jnp.zeros((d,), jnp.float32), 'bn2_m': jnp.zeros((d,), jnp.float32), 'bn2_v': jnp.ones((d,), jnp.float32), 'w_msg': jax.random.normal(ks[4], (d, d), jnp.float32) * s, 'b_msg': jnp.zeros((d,), jnp.float32), 'w_ih': jax.random.normal(ks[5], (3 * d, 2 * d), jnp.float32) * s, 'b_ih': jnp.zeros((3 * d,), jnp.float32), 'w_hh': jax.random.normal(ks[6], (3 * d, d), jnp.float32) * s, 'b_hh': jnp.zeros((3 * d,), jnp.float32)}
    _L1_gnn_all = _L1_gnn_setup()
    _L1_gnn_in = {k: v for k, v in _L1_gnn_all.items() if k in ('w_se', 'b_se', 'conv1_w', 'bn1_g', 'bn1_b', 'bn1_m', 'bn1_v', 'conv2_w', 'bn2_g', 'bn2_b', 'bn2_m', 'bn2_v', 'w_msg', 'b_msg', 'w_ih', 'b_ih', 'w_hh', 'b_hh')}
    del _L1_gnn_all

    def _L1_ffn_setup():
        import jax, jax.numpy as jnp
        import numpy as np
        C = 128
        EPS = 1e-05
        N_ITERS = 30

        def _layernorm(x, w, bias):
            mu = jnp.mean(x, axis=-1, keepdims=True)
            var = jnp.mean(jnp.square(x - mu), axis=-1, keepdims=True)
            return (x - mu) * jax.lax.rsqrt(var + EPS) * w + bias
        key = jax.random.key(seed)
        kx, kw, kb, klw, klb = jax.random.split(key, 5)
        x = jax.random.normal(kx, (8, 1024, C), dtype=jnp.float32)
        bound = 1.0 / np.sqrt(C)
        W = jax.random.uniform(kw, (C, C), minval=-bound, maxval=bound, dtype=jnp.float32)
        b = jax.random.uniform(kb, (C,), minval=-bound, maxval=bound, dtype=jnp.float32)
        ln_w = jnp.ones((C,), dtype=jnp.float32)
        ln_b = jnp.zeros((C,), dtype=jnp.float32)
        return {'x': x, 'ln_w': ln_w, 'ln_b': ln_b, 'W': W, 'b': b}
    _L1_ffn_all = _L1_ffn_setup()
    _L1_ffn_in = {k: v for k, v in _L1_ffn_all.items() if k in ('ln_w', 'ln_b', 'W', 'b')}
    del _L1_ffn_all
    return {'x': x, 'adj': adj, 'L0_gnn_W': _L0_gnn_in['W'], 'L0_gnn_b': _L0_gnn_in['b'], 'L0_ffn_weight': _L0_ffn_in['weight'], 'L0_ffn_bias': _L0_ffn_in['bias'], 'L1_gnn_w_se': _L1_gnn_in['w_se'], 'L1_gnn_b_se': _L1_gnn_in['b_se'], 'L1_gnn_conv1_w': _L1_gnn_in['conv1_w'], 'L1_gnn_bn1_g': _L1_gnn_in['bn1_g'], 'L1_gnn_bn1_b': _L1_gnn_in['bn1_b'], 'L1_gnn_bn1_m': _L1_gnn_in['bn1_m'], 'L1_gnn_bn1_v': _L1_gnn_in['bn1_v'], 'L1_gnn_conv2_w': _L1_gnn_in['conv2_w'], 'L1_gnn_bn2_g': _L1_gnn_in['bn2_g'], 'L1_gnn_bn2_b': _L1_gnn_in['bn2_b'], 'L1_gnn_bn2_m': _L1_gnn_in['bn2_m'], 'L1_gnn_bn2_v': _L1_gnn_in['bn2_v'], 'L1_gnn_w_msg': _L1_gnn_in['w_msg'], 'L1_gnn_b_msg': _L1_gnn_in['b_msg'], 'L1_gnn_w_ih': _L1_gnn_in['w_ih'], 'L1_gnn_b_ih': _L1_gnn_in['b_ih'], 'L1_gnn_w_hh': _L1_gnn_in['w_hh'], 'L1_gnn_b_hh': _L1_gnn_in['b_hh'], 'L1_ffn_ln_w': _L1_ffn_in['ln_w'], 'L1_ffn_ln_b': _L1_ffn_in['ln_b'], 'L1_ffn_W': _L1_ffn_in['W'], 'L1_ffn_b': _L1_ffn_in['b']}

def reference(x, adj, L0_gnn_W, L0_gnn_b, L0_ffn_weight, L0_ffn_bias, L1_gnn_w_se, L1_gnn_b_se, L1_gnn_conv1_w, L1_gnn_bn1_g, L1_gnn_bn1_b, L1_gnn_bn1_m, L1_gnn_bn1_v, L1_gnn_conv2_w, L1_gnn_bn2_g, L1_gnn_bn2_b, L1_gnn_bn2_m, L1_gnn_bn2_v, L1_gnn_w_msg, L1_gnn_b_msg, L1_gnn_w_ih, L1_gnn_b_ih, L1_gnn_w_hh, L1_gnn_b_hh, L1_ffn_ln_w, L1_ffn_ln_b, L1_ffn_W, L1_ffn_b):
    import jax
    import jax.numpy as jnp

    def _L0_gnn_ref(node_features, adj_matrix, W, b):
        import jax, jax.numpy as jnp
        import numpy as np
        B, N, F_IN, F_OUT = (8, 1024, 128, 128)
        degree = jnp.sum(adj_matrix, axis=-1)
        d_inv_sqrt = jnp.power(degree, -0.5)
        d_inv_sqrt = jnp.where(jnp.isinf(d_inv_sqrt), 0.0, d_inv_sqrt)
        norm_adj = adj_matrix * d_inv_sqrt[:, :, None] * d_inv_sqrt[:, None, :]
        transformed = jnp.einsum('bnf,of->bno', node_features, W) + b
        output = jnp.einsum('bnm,bmo->bno', norm_adj, transformed)
        return jax.nn.relu(output)

    def _L0_ffn_ref(x, weight, bias):
        import jax, jax.numpy as jnp
        import numpy as np
        IN_CH = 128
        OUT_CH = 128
        return jnp.einsum('bsi,oi->bso', x, weight) + bias

    def _L1_gnn_ref(x, mask, w_se, b_se, conv1_w, bn1_g, bn1_b, bn1_m, bn1_v, conv2_w, bn2_g, bn2_b, bn2_m, bn2_v, w_msg, b_msg, w_ih, b_ih, w_hh, b_hh):
        import jax, jax.numpy as jnp
        import numpy as np
        from jax import lax
        DIM = 128
        EPS = 1e-05

        def _bn(h, g, b, m, v):
            scale = g / jnp.sqrt(v + EPS)
            return h * scale[None, :, None] + (b - m * scale)[None, :, None]

        def _conv1d(h, w, pad):
            return lax.conv_general_dilated(h, w, window_strides=(1,), padding=[(pad, pad)], dimension_numbers=('NCH', 'OIH', 'NCH'))
        d = x.shape[-1]
        xc = jnp.transpose(x, (0, 2, 1))
        h = _bn(_conv1d(xc, conv1_w, 0), bn1_g, bn1_b, bn1_m, bn1_v)
        h = jax.nn.relu(h)
        h = _bn(_conv1d(h, conv2_w, 8), bn2_g, bn2_b, bn2_m, bn2_v)
        x_conv = jnp.transpose(jax.nn.relu(h + xc), (0, 2, 1))
        s = x @ w_se.T + b_se
        sq = jnp.sum(s * s, axis=-1)
        dist = sq[:, :, None] + sq[:, None, :] - 2.0 * jnp.einsum('bnd,bmd->bnm', s, s)
        A = jnp.exp(-dist) * mask
        msg = jax.nn.relu(x @ w_msg.T + b_msg)
        x_nmp = jnp.einsum('bnm,bmd->bnd', A, msg)
        x_in = jnp.concatenate([x_conv, x_nmp], axis=-1)
        gi = x_in @ w_ih.T + b_ih
        gh = x @ w_hh.T + b_hh
        gi_r, gi_z, gi_n = (gi[..., :d], gi[..., d:2 * d], gi[..., 2 * d:])
        gh_r, gh_z, gh_n = (gh[..., :d], gh[..., d:2 * d], gh[..., 2 * d:])
        r = jax.nn.sigmoid(gi_r + gh_r)
        z = jax.nn.sigmoid(gi_z + gh_z)
        nn_ = jnp.tanh(gi_n + r * gh_n)
        return (1.0 - z) * nn_ + z * x

    def _L1_ffn_ref(x, ln_w, ln_b, W, b):
        import jax, jax.numpy as jnp
        import numpy as np
        C = 128
        EPS = 1e-05
        N_ITERS = 30

        def _layernorm(x, w, bias):
            mu = jnp.mean(x, axis=-1, keepdims=True)
            var = jnp.mean(jnp.square(x - mu), axis=-1, keepdims=True)
            return (x - mu) * jax.lax.rsqrt(var + EPS) * w + bias

        def step(h, _):
            h = h + 0.01 * jnp.tanh(h)
            h = h * jax.nn.sigmoid(h)
            h = _layernorm(h, ln_w, ln_b)
            h = jnp.einsum('bsc,dc->bsd', h, W) + b
            return (h, None)
        x, _ = jax.lax.scan(step, x, None, length=N_ITERS)
        return x
    x = x + _L0_gnn_ref(_layernorm(x, axis=-1), adj, L0_gnn_W, L0_gnn_b)
    x = x + _L0_ffn_ref(_layernorm(x, axis=-1), L0_ffn_weight, L0_ffn_bias)
    x = x + _L1_gnn_ref(_layernorm(x, axis=-1), adj, L1_gnn_w_se, L1_gnn_b_se, L1_gnn_conv1_w, L1_gnn_bn1_g, L1_gnn_bn1_b, L1_gnn_bn1_m, L1_gnn_bn1_v, L1_gnn_conv2_w, L1_gnn_bn2_g, L1_gnn_bn2_b, L1_gnn_bn2_m, L1_gnn_bn2_v, L1_gnn_w_msg, L1_gnn_b_msg, L1_gnn_w_ih, L1_gnn_b_ih, L1_gnn_w_hh, L1_gnn_b_hh)
    x = x + _L1_ffn_ref(_layernorm(x, axis=-1), L1_ffn_ln_w, L1_ffn_ln_b, L1_ffn_W, L1_ffn_b)
    return x

_drawn_inputs = setup_inputs


def setup_inputs(seed=0):
    import zlib

    import numpy as np

    out = dict(_drawn_inputs(seed))
    spreads = {'L1_gnn_b_se': (0.0, 0.8),
     'L1_gnn_bn1_g': (1.0, 0.2),
     'L1_gnn_bn1_b': (0.0, 0.309),
     'L1_gnn_bn1_m': (0.0, 0.282),
     'L1_gnn_bn1_v': (1.0, 0.6),
     'L1_gnn_bn2_g': (1.0, 0.2),
     'L1_gnn_bn2_b': (0.0, 0.525),
     'L1_gnn_bn2_m': (0.0, 0.435),
     'L1_gnn_bn2_v': (1.0, 0.6),
     'L1_gnn_b_msg': (0.0, 0.1),
     'L1_gnn_b_ih': (0.0, 0.1),
     'L1_gnn_b_hh': (0.0, 0.273),
     'L1_ffn_ln_w': (1.0, 0.2),
     'L1_ffn_ln_b': (0.0, 0.1)}
    factors = {}
    for name, (base, spread) in spreads.items():
        noise = np.random.default_rng([zlib.crc32(name.encode()), seed]).standard_normal(out[name].shape)
        drawn = base * np.exp(spread * noise) if base else spread * noise
        out[name] = jnp.asarray(drawn.astype(out[name].dtype))
    for name, factor in factors.items():
        out[name] = (out[name] * factor).astype(out[name].dtype)
    return out
```

```python
from contextlib import ExitStack

import concourse.bass as bass
from concourse import mybir

F32 = mybir.dt.float32
BF16 = mybir.dt.bfloat16
ALU = mybir.AluOpType
ACT = mybir.ActivationFunctionType
AX_X = mybir.AxisListType.X

P = 128
B, N, C = 16, 512, 128
NT = N // P
TAPS = 17
HALO = TAPS // 2
EPS = 1e-5
ITERS = 30
STEP = 0.01
GT = 8
GROUPS = B * NT // GT
GN = GT * P
NSE = 3
KD = 64 + NSE
LAG_S = 2
LAG_V = 3
LAG_P = 4
LAG_A = 5
LAG_T = 7
ACT_TILES = 1


def wait(eng, sem, count):
    if not isinstance(count, int) or count > 0:
        eng.wait_ge(sem, count)


def settle(eng, passed):
    eng.sem_inc(passed, 1)


def tiles(ap):
    return ap.rearrange("p (t c) -> p t c", c=C)


def spread(col, n, width):
    return col.rearrange("p (t o) -> p t o", o=1).broadcast_to([P, n, width])


def build(nc, x, adj, w0, b0, wf, bf, w_se, b_se, conv1_w, bn1, conv2_w, bn2, w_msg, b_msg,
          w_ih, b_ih, w_hh, b_hh, ln_w, ln_b, w1, b1, out):
    with ExitStack() as ctx:
        def sb(name, shape, dt=F32):
            return ctx.enter_context(nc.sbuf_tensor(name, shape, dt))

        def sem(name):
            return ctx.enter_context(nc.semaphore(name))

        x_tok = sb("x_tok", [P, B * NT, C])
        y_all = sb("y_all", [P, B * NT, C])
        work = sb("work", [P, 24 * N])

        def piece(first, count):
            return work[:, first * N:(first + count) * N]

        adj_in = [piece(4 * p, 4).rearrange("p (t m) -> p t m", m=N) for p in range(2)]
        adj_t = [piece(8 + 4 * p, 4).rearrange("p (t n) -> p t n", n=N) for p in range(2)]
        edge = piece(16, 4).rearrange("p (t n) -> p t n", n=N)
        t_ring = [piece(2 * r, 2) for r in range(2)]
        u_ring = [piece(4 + 2 * r, 2) for r in range(2)]
        g_ring = [piece(8 + 2 * r, 2) for r in range(4)]
        h_ring = [piece(16 + 2 * r, 2) for r in range(4)]
        conv2_nat = work[:, 0:C * TAPS].rearrange("p (i k) -> p i k", k=TAPS)
        nat = tiles(piece(16, 4))
        wt = sb("wt", [P, 15 + TAPS, C])
        CONV2, W0, WF, W1 = 0, TAPS, TAPS + 1, TAPS + 2
        IH, HH, MSG, CONV1, WSE = TAPS + 3, TAPS + 9, TAPS + 12, TAPS + 13, TAPS + 14
        wse = sb("wse", [P, KD])
        ident = sb("ident", [P, P])
        ones_bf = sb("ones_bf", [KD, P], BF16)
        bias1 = sb("bias1", [KD, NT, C], BF16)
        part_bf = sb("part_bf", [KD, 3, C], BF16)
        part_f = sb("part_f", [KD, 3, C])
        bcol = sb("bcol", [P, 32])
        lnw_row = sb("lnw_row", [P, C])
        lnb_row = sb("lnb_row", [P, C])
        bmsg_row = sb("bmsg_row", [P, C])
        se_bias = sb("se_bias", [KD, 1])
        se_bias2 = sb("se_bias2", [KD, 1])
        half_neg = sb("half_neg", [P, 8])
        tmp_w = sb("tmp_w", [P, C])
        b1_cols = sb("b1_cols", [P, KD])

        ln_stat = sb("ln_stat", [P, 4, NT, 6])
        ln_mv = sb("ln_mv", [P, 4, NT, 2])
        ln_ve = sb("ln_ve", [P, 4, NT])
        ln_rs = sb("ln_rs", [P, 4, NT])
        xh = sb("xh", [P, 3, NT, C])
        xh0_t = sb("xh0_t", [P, N])
        xh1_t = sb("xh1_t", [P, N])
        xc = [sb(f"xc{p}", [P, N]) for p in range(2)]
        deg = sb("deg", [P, NT])
        deg0 = sb("deg0", [P, 3, NT])
        dinv = sb("dinv", [P, NT])
        t_tok = sb("t_tok", [P, NT, C])
        agg_tok = sb("agg_tok", [P, NT, C])
        h_pad = sb("h_pad", [P, N + 2 * HALO])
        emb_m = sb("emb_m", [KD, N])
        emb_n = sb("emb_n", [KD, N])
        msg_pre = sb("msg_pre", [P, NT, C])
        msg_tok = sb("msg_tok", [P, NT, C])
        conv_pre = sb("conv_pre", [P, N])
        x_conv = sb("x_conv", [P, N])
        x_nmp = sb("x_nmp", [P, N])
        gate_r = sb("gate_r", [P, N])
        gate_z = sb("gate_z", [P, N])
        gh_n = sb("gh_n", [P, N])
        rh = sb("rh", [P, N])
        n_pre = sb("n_pre", [P, N])
        n_act = sb("n_act", [P, N])
        x_less_n = sb("x_less_n", [P, N])
        z_part = sb("z_part", [P, N])
        upd = sb("upd", [P, N])
        f_stat = sb("f_stat", [P, 2, GT, 6])
        f_small = sb("f_small", [P, 3, GT])
        f_var = sb("f_var", [P, 2, GT])
        f_rs = sb("f_rs", [P, 4, GT])

        psum = ctx.enter_context(nc.psum_tensor("psum", [P, 8, N], F32))
        bank = [psum[:, i, :] for i in range(8)]
        TURN_A, TURN_B, TURN_X, TOK, CONV, CHAN, DIST_A, DIST_B = range(8)
        y_ps = [psum[:, 2 * r:2 * r + 2, :] for r in range(2)]
        g_ps = [psum[:, 4 + 2 * r:6 + 2 * r, :] for r in range(2)]

        s_small = sem("s_small")
        s_wload = sem("s_wload")
        s_const = sem("s_const")
        s_ident = sem("s_ident")
        s_fold = sem("s_fold")
        s_folded = sem("s_folded")
        s_pow = sem("s_pow")
        s_wturn = sem("s_wturn")
        s_wcopy = sem("s_wcopy")
        s_brow = sem("s_brow")
        s_ready = sem("s_ready")
        s_in = [sem(f"s_in{p}") for p in range(2)]
        s_adj_turned = sem("s_adj_turned")
        s_adjt_even = sem("s_adjt_even")
        s_adjt_odd = sem("s_adjt_odd")
        s_deg = sem("s_deg")
        s_dinv = sem("s_dinv")
        s_stat = [sem(f"s_stat{w}") for w in range(4)]
        s_mv = [sem(f"s_mv{w}") for w in range(4)]
        s_rs = [sem(f"s_rs{w}") for w in range(4)]
        s_norm = [sem(f"s_norm{w}") for w in range(4)]
        s_turn = [sem(f"s_turn{w}") for w in range(3)]
        s_xt = [sem(f"s_xt{w}") for w in range(3)]
        s_t = sem("s_t")
        s_t_scaled = sem("s_t_scaled")
        s_agg = sem("s_agg")
        s_agg_scaled = sem("s_agg_scaled")
        s_x1 = sem("s_x1")
        s_ffn = sem("s_ffn")
        s_x2 = sem("s_x2")
        s_conv1 = sem("s_conv1")
        s_h1 = sem("s_h1")
        s_emb = sem("s_emb")
        s_emb_parts = sem("s_emb_parts")
        s_msg = sem("s_msg")
        s_msg_pre = sem("s_msg_pre")
        s_msg_tok = sem("s_msg_tok")
        s_conv2 = sem("s_conv2")
        s_conv_pre = sem("s_conv_pre")
        s_x_conv = sem("s_x_conv")
        s_dist = sem("s_dist")
        s_exp = sem("s_exp")
        s_edge_p = sem("s_edge_p")
        s_edge_v = sem("s_edge_v")
        s_nmp = sem("s_nmp")
        s_x_nmp = sem("s_x_nmp")
        s_ghn_ps = sem("s_ghn_ps")
        s_gh_n = sem("s_gh_n")
        s_r_ps = sem("s_r_ps")
        s_r = sem("s_r")
        s_z_ps = sem("s_z_ps")
        s_z = sem("s_z")
        s_gin_ps = sem("s_gin_ps")
        s_rh = sem("s_rh")
        s_n_pre = sem("s_n_pre")
        s_n = sem("s_n")
        s_x_less_n = sem("s_x_less_n")
        s_z_part = sem("s_z_part")
        s_upd = sem("s_upd")
        s_back = sem("s_back")
        s_x3 = sem("s_x3")
        f_mm = sem("f_mm")
        f_tanh = sem("f_tanh")
        f_u = sem("f_u")
        f_silu = sem("f_silu")
        f_bn = sem("f_bn")
        f_sm = sem("f_sm")
        f_v = sem("f_v")
        f_pow = sem("f_pow")
        f_norm = sem("f_norm")
        f_norm_act = sem("f_norm_act")
        f_turn = sem("f_turn")
        f_state = sem("f_state")
        f_out = sem("f_out")
        s_store = sem("s_store")
        s_passed_sp = sem("s_passed_sp")
        s_passed_pool = sem("s_passed_pool")
        s_passed_dve = sem("s_passed_dve")

        block = ctx.enter_context(nc.Block())

        def graph(b):
            return bass.ds(b * NT, NT)

        x_dram = x.rearrange("b (t p) c -> b p t c", p=P)
        adj_dram = adj.rearrange("b (t p) m -> b p t m", p=P)
        out_dram = out.rearrange("b (t p) c -> p (b t) c", p=P)

        def col(v):
            return v.rearrange("(p o) -> p o", o=1)

        (B0, BF, B1, G1, BE1, M1, V1, G2, BE2, M2, V2, BR, BZ, BN_, HR, HZ, HN,
         SC1, SH1, SC2, SH2, RZB, ZZB, HNB, T0, T1, FB1) = range(27)
        small = [(b0, B0), (bf, BF), (b1, B1)] + list(zip(bn1, (G1, BE1, M1, V1))) + \
            list(zip(bn2, (G2, BE2, M2, V2))) + \
            [(b_ih[C * j:C * j + C], BR + j) for j in range(3)] + [(b_hh[C * j:C * j + C], HR + j) for j in range(3)]
        NSMALL = len(small) + 3 + 3
        weights = [(conv2_nat, conv2_w), (nat[:, 0, :], w0), (nat[:, 1, :], wf), (nat[:, 2, :], w1)] + \
            [(nat[:, 3 + 2 * j:5 + 2 * j, :], w_ih[C * j:C * j + C, :].rearrange("o (h i) -> o h i", h=2)) for j in range(3)] + \
            [(nat[:, 9 + j, :], w_hh[C * j:C * j + C, :]) for j in range(3)] + \
            [(nat[:, 12, :], w_msg), (nat[:, 13, :], conv1_w.rearrange("o i k -> o (i k)")), (nat[0:NSE, 14, :], w_se)]
        NWEIGHTS = len(weights)

        def steps(eng, step):
            step(None, 1, 0)
            for b in range(2):
                step(b, b % 2, b + 1)
            with eng.Fori(1, B // 2 - 1) as i:
                for p in range(2):
                    step(i * 2 + p, p, i * 2 + (p + 1))
            for b in range(B - 2, B):
                step(b, b % 2, b + 1 if b + 1 < B else None)
            step(B, 0, None)

        def slots(eng, slot):
            for k in range(GROUPS):
                slot(0, k)
            with eng.Fori(1, ITERS) as it:
                for k in range(GROUPS):
                    slot(it, k)
            for k in range(GROUPS):
                slot(ITERS, k)

        def loaded(c, q):
            return (c + 2 - q) * 16

        def later(b):
            return b is not None and not (isinstance(b, int) and b == 0)

        def exists(b):
            return b is not None and not (isinstance(b, int) and b == B)

        def earlier(it, k, lag):
            if k >= lag:
                if isinstance(it, int) and it == ITERS:
                    return None
                return it, k - lag, it * GROUPS + (k - lag)
            if isinstance(it, int) and it == 0:
                return None
            return it - 1, k - lag + GROUPS, (it - 1) * GROUPS + (k - lag + GROUPS)

        @block.sync
        def _(sp):
            for dst, src in weights:
                sp.dma_start(dst, src).then_inc(s_wload, 16)
            for v, c in small:
                sp.dma_start(bcol[:, c:c + 1], col(v)).then_inc(s_small, 16)
            for r in range(3):
                sp.dma_start(se_bias[32 * r:32 * r + NSE, :], col(b_se)).then_inc(s_small, 16)
            for row, v in ((lnw_row, ln_w), (lnb_row, ln_b), (bmsg_row, b_msg)):
                sp.dma_start(row[:], v.rearrange("(o c) -> o c", o=1).broadcast_to([P, C])).then_inc(s_small, 16)

            def load(b, p):
                wait(sp, s_adj_turned, 4 * (b - 1))
                settle(sp, s_passed_sp)
                wait(sp, s_deg, 3 * (b - 1))
                settle(sp, s_passed_sp)
                sp.dma_start(adj_in[p], adj_dram[b]).then_inc(s_in[p], 16)
                sp.dma_start(x_tok[:, graph(b), :], x_dram[b]).then_inc(s_in[p], 16)

            sp.wait_ge(s_wturn, 5)
            load(0, 0)
            load(1, 1)
            with sp.Fori(1, B // 2) as i:
                for p in range(2):
                    load(i * 2 + p, p)
            for k in range(GROUPS):
                sp.wait_ge(f_out, k + 1)
                sp.dma_start(out_dram[:, GT * k:GT * k + GT, :], y_all[:, GT * k:GT * k + GT, :]).then_inc(s_store, 16)
            sp.wait_ge(s_store, 16 * GROUPS)

        @block.gpsimd
        def _(pool):
            pool.wait_ge(s_const, 1)
            pool.affine_select(out=ident[:], in_=ident[:], compare_op=ALU.is_equal, fill=0.0, base=0,
                               pattern=[[-1, P]], channel_multiplier=1).then_inc(s_ident, 1)
            pool.wait_ge(s_small, 16 * NSMALL)
            pool.tensor_scalar(bcol[:, T0:T0 + 1], bcol[:, V1:V1 + 1], 1.0, EPS, ALU.mult, ALU.add)
            pool.tensor_scalar(bcol[:, T1:T1 + 1], bcol[:, V2:V2 + 1], 1.0, EPS, ALU.mult, ALU.add).then_inc(s_pow, 1)
            pool.wait_ge(s_pow, 1)
            pool.tensor_tensor(bcol[:, SC1:SC1 + 1], bcol[:, T0:T0 + 1], half_neg[:, 0:1], ALU.pow)
            pool.tensor_tensor(bcol[:, SC2:SC2 + 1], bcol[:, T1:T1 + 1], half_neg[:, 0:1], ALU.pow).then_inc(s_pow, 1)

            def rstd(w, n):
                pool.wait_ge(s_mv[w], n + 1)
                settle(pool, s_passed_pool)
                pool.tensor_scalar(ln_ve[:, w, :], ln_mv[:, w, :, 1], 1.0, EPS, ALU.mult, ALU.add).then_inc(s_rs[w], 1)
                pool.wait_ge(s_rs[w], 2 * n + 1)
                pool.tensor_tensor(ln_rs[:, w, :], ln_ve[:, w, :], half_neg[:, 0:NT], ALU.pow).then_inc(s_rs[w], 1)

            def edges(b, p, mt):
                pool.wait_ge(s_exp, 4 * b + mt + 1)
                pool.tensor_tensor(edge[:, mt, :], edge[:, mt, :], adj_t[p][:, mt, :], ALU.mult).then_inc(s_edge_p, 1)

            def step(b, p, c):
                l1 = exists(b)
                if c is not None:
                    rstd(0, c)
                    pool.wait_ge(s_deg, 3 * c + 3)
                    wait(pool, s_x1, c)
                    pool.tensor_tensor(deg0[:, 2, :], deg0[:, 1, :], half_neg[:, 0:NT], ALU.pow).then_inc(s_dinv, 1)
                    pool.wait_ge(s_dinv, 2 * c + 1)
                    pool.tensor_tensor(dinv[:], deg0[:, 2, :], deg0[:, 0, :], ALU.mult).then_inc(s_dinv, 1)
                if l1:
                    pool.wait_ge(s_msg_pre, b + 1)
                    wait(pool, s_nmp, b)
                    settle(pool, s_passed_pool)
                    pool.tensor_scalar(msg_tok[:], msg_pre[:], 0.0, None, ALU.max).then_inc(s_msg_tok, 1)
                if later(b):
                    rstd(3, b - 1)
                if l1:
                    edges(b, p, 0)
                if c is not None:
                    rstd(1, c)
                if l1:
                    edges(b, p, 2)
                if c is not None:
                    rstd(2, c)

            steps(pool, step)

            def slot(it, k):
                before = earlier(it, k, LAG_P)
                if before is None:
                    return
                _, j, s = before
                pool.wait_ge(f_v, s + 1)
                wait(pool, f_norm_act, s - 3)
                pool.tensor_tensor(f_rs[:, j % 4, :], f_var[:, j % 2, :], half_neg[:, 0:GT], ALU.pow).then_inc(f_pow, 1)
                pool.wait_ge(f_pow, s + 1)
                wait(pool, f_turn, s - 3)
                t = GT - ACT_TILES
                pool.tensor_tensor(tiles(h_ring[j % 4])[:, 0:t, :], tiles(g_ring[j % 4])[:, 0:t, :],
                                   spread(f_rs[:, j % 4, 0:t], t, C), ALU.mult).then_inc(f_norm, 1)

            slots(pool, slot)

        @block.tensor
        def _(pe):
            pe.wait_ge(s_ident, 1)
            pe.wait_ge(s_folded, 1)
            pe.wait_ge(s_wload, 16 * NWEIGHTS)
            for j in range(TAPS + 15):
                if j < TAPS:
                    src, rows = conv2_nat[:, :, j], P
                elif j == WSE:
                    src, rows = nat[0:NSE, j - TAPS, :], NSE
                else:
                    src, rows = nat[:, j - TAPS, :], P
                m = pe.transpose(psum[:, j // 4, C * (j % 4):C * (j % 4) + rows], src, ident[0:rows, 0:rows])
                if j % 4 == 3:
                    m.then_inc(s_wturn, 1)
            pe.wait_ge(s_wcopy, 8)
            pe.wait_ge(s_brow, 1)
            pe.matmul(psum[0:KD, 0, 0:C], b1_cols[:], ident[:], start=True, stop=True).then_inc(s_brow, 1)
            pe.wait_ge(s_ready, 1)

            def w(j):
                return wt[:, j, :]

            def turn(k, n):
                pe.wait_ge(s_norm[k], n + 1)
                for t in range(NT):
                    m = pe.transpose(bank[TURN_X][:, P * t:P * t + P], xh[:, k, t, :], ident[:])
                m.then_inc(s_turn[k], 1)

            def tokens(lhs, rhs, done):
                for t in range(NT):
                    m = pe.matmul(bank[TOK][:, C * t:C * t + C], lhs[:, P * t:P * t + P], rhs, start=True, stop=True)
                m.then_inc(done, 1)

            def adj_turn(c, p, mt):
                bk = bank[TURN_A if mt % 2 == 0 else TURN_B]
                for t in range(NT):
                    m = pe.transpose(bk[:, P * t:P * t + P], adj_in[p][:, t, P * mt:P * mt + P], ident[:])
                m.then_inc(s_adj_turned, 1)

            def step(b, p, c):
                q = 1 - p
                l1 = exists(b)
                l0 = c is not None

                def conv2(first, last):
                    if not l1:
                        return
                    if first == 0:
                        pe.wait_ge(s_h1, b + 1)
                        wait(pe, s_conv_pre, b)
                    for k in range(first, last):
                        m = pe.matmul(bank[CONV], w(CONV2 + k), h_pad[:, k:k + N], start=(k == 0), stop=(k == TAPS - 1))
                    if last == TAPS:
                        m.then_inc(s_conv2, 1)

                def dist(mt):
                    if not l1:
                        return
                    if mt == 0:
                        pe.wait_ge(s_emb_parts, 4 * b + 4)
                        wait(pe, s_r, b)
                    if mt == 1:
                        wait(pe, s_z, b)
                    if mt >= 2:
                        pe.wait_ge(s_exp, 4 * b + mt - 1)
                    pe.matmul(bank[DIST_A + mt % 2], emb_m[:, P * mt:P * mt + P], emb_n[:],
                              start=True, stop=True).then_inc(s_dist, 1)

                if l1:
                    pe.wait_ge(s_xt[2], b + 1)
                    wait(pe, s_x_nmp, b)
                    pe.matmul(bank[CHAN], w(CONV1), xc[p][:], start=True, stop=True).then_inc(s_conv1, 1)
                    pe.wait_ge(s_x2, b + 1)
                    tokens(xc[p], w(MSG), s_msg)
                    pe.wait_ge(s_h1, b + 1)
                    pe.matmul(bank[CHAN][0:KD, :], wse[:], xc[p][:], start=True, stop=True).then_inc(s_emb, 1)
                if l0:
                    pe.wait_ge(s_in[q], loaded(c, q))
                    if b is not None:
                        wait(pe, s_n_pre, b)
                    adj_turn(c, q, 0)
                    if b is not None:
                        wait(pe, s_gh_n, b)
                    adj_turn(c, q, 1)
                conv2(0, 3)
                if later(b):
                    pe.wait_ge(s_upd, b)
                    if l1:
                        pe.wait_ge(s_xt[2], b + 1)
                    for t in range(NT):
                        m = pe.transpose(bank[TURN_X][:, C * t:C * t + C], upd[:, P * t:P * t + P], ident[:])
                    m.then_inc(s_back, 1)
                if l0:
                    pe.wait_ge(s_adjt_even, 2 * c + 1)
                    adj_turn(c, q, 2)
                    pe.wait_ge(s_adjt_odd, 2 * c + 1)
                    adj_turn(c, q, 3)
                conv2(3, 6)
                if l0:
                    if b is not None:
                        wait(pe, s_x3, b)
                    turn(0, c)
                conv2(6, 9)
                if l0:
                    pe.wait_ge(s_xt[0], c + 1)
                    if l1:
                        pe.wait_ge(s_msg_pre, b + 1)
                    tokens(xh0_t, w(W0), s_t)
                dist(0)
                dist(1)
                if l0:
                    pe.wait_ge(s_t_scaled, c + 1)
                    pe.wait_ge(s_adjt_even, 2 * c + 2)
                    pe.wait_ge(s_adjt_odd, 2 * c + 2)
                    for t in range(NT):
                        for mt in range(NT):
                            m = pe.matmul(bank[TOK][:, C * t:C * t + C], adj_t[q][:, mt, P * t:P * t + P],
                                          t_tok[:, mt, :], start=(mt == 0), stop=(mt == NT - 1))
                    m.then_inc(s_agg, 1)
                conv2(9, 12)
                dist(2)
                dist(3)
                conv2(12, 15)
                if l0:
                    pe.wait_ge(s_xt[0], c + 1)
                    turn(1, c)
                conv2(15, TAPS)
                if l0:
                    pe.wait_ge(s_xt[1], c + 1)
                    pe.wait_ge(s_agg_scaled, c + 1)
                    tokens(xh1_t, w(WF), s_ffn)
                if l1:
                    pe.wait_ge(s_msg_tok, b + 1)
                    for mt in range(NT):
                        if mt % 2 == 0:
                            pe.wait_ge(s_edge_p, 2 * b + mt // 2 + 1)
                        else:
                            pe.wait_ge(s_edge_v, 2 * b + mt // 2 + 1)
                        m = pe.matmul(bank[CHAN], msg_tok[:, mt, :], edge[:, mt, :], start=(mt == 0), stop=(mt == NT - 1))
                    m.then_inc(s_nmp, 1)
                    if l0:
                        pe.wait_ge(s_adjt_odd, 2 * c + 2)
                    else:
                        pe.wait_ge(s_gh_n, b)
                    pe.matmul(bank[TURN_B], w(HH + 2), xc[p][:], start=True, stop=True).then_inc(s_ghn_ps, 1)
                    pe.wait_ge(s_exp, 4 * b + 4)
                    pe.matmul(bank[DIST_A], w(HH), xc[p][:], start=True, stop=False)
                    pe.matmul(bank[DIST_B], w(HH + 1), xc[p][:], start=True, stop=False)
                    pe.wait_ge(s_x_conv, b + 1)
                    pe.matmul(bank[DIST_A], w(IH), x_conv[:], start=False, stop=False)
                    pe.matmul(bank[DIST_B], w(IH + 2), x_conv[:], start=False, stop=False)
                if l0:
                    pe.wait_ge(s_xt[1], c + 1)
                    turn(2, c)
                if l1:
                    pe.wait_ge(s_x_nmp, b + 1)
                    pe.matmul(bank[DIST_A], w(IH + 1), x_nmp[:], start=False, stop=True).then_inc(s_r_ps, 1)
                    if l0:
                        pe.wait_ge(s_adjt_even, 2 * c + 2)
                    else:
                        pe.wait_ge(s_n_pre, b)
                    pe.matmul(bank[TURN_A], w(IH + 4), x_conv[:], start=True, stop=False)
                    pe.matmul(bank[TURN_A], w(IH + 5), x_nmp[:], start=False, stop=True).then_inc(s_gin_ps, 1)
                    pe.matmul(bank[DIST_B], w(IH + 3), x_nmp[:], start=False, stop=True).then_inc(s_z_ps, 1)

            steps(pe, step)

            def slot(it, k):
                before = earlier(it, k, LAG_T)
                if before is not None:
                    _, j, s = before
                    pe.wait_ge(f_norm, s + 1)
                    pe.wait_ge(f_norm_act, s + 1)
                    wait(pe, f_state, s - 1)
                    for t in range(GT):
                        m = pe.transpose(g_ps[j % 2][:, t // NT, P * (t % NT):P * (t % NT) + P],
                                         tiles(h_ring[j % 4])[:, t, :], ident[:])
                    m.then_inc(f_turn, 1)
                if not (isinstance(it, int) and it == 0):
                    s = (it - 1) * GROUPS + k
                    pe.wait_ge(f_state, s + 1)
                    if isinstance(it, int) and it == ITERS:
                        if k >= 2:
                            pe.wait_ge(f_out, k - 1)
                        else:
                            pe.wait_ge(f_u, ITERS * GROUPS - 1 + k)
                    else:
                        pe.wait_ge(f_u, s + GROUPS - 1)
                    for h in range(2):
                        pe.matmul(y_ps[k % 2][:, h, :], ones_bf[:], bias1[:].rearrange("p t c -> p (t c)"),
                                  start=True, stop=False, skip_group_check=True)
                        for t in range(NT):
                            m = pe.matmul(y_ps[k % 2][:, h, C * t:C * t + C], y_all[:, GT * k + NT * h + t, :], w(W1),
                                          start=False, stop=True, skip_group_check=True)
                    m.then_inc(f_mm, 1)

            slots(pe, slot)


        @block.scalar
        def _(act):
            act.wait_ge(s_ready, 1)

            def vec(c):
                return bcol[:, c:c + 1]

            def adjt_even(c, q, mt):
                act.wait_ge(s_adj_turned, 4 * c + mt + 1)
                wait(act, s_edge_p, 2 * (c - 1))
                wait(act, s_edge_v, 2 * (c - 1))
                act.activation(adj_t[q][:, mt, :], bank[TURN_A], ACT.Copy).then_inc(s_adjt_even, 1)

            def exp(b, mt):
                act.wait_ge(s_dist, 4 * b + mt + 1)
                wait(act, s_nmp, b)
                act.activation(edge[:, mt, :], bank[DIST_A + mt % 2], ACT.Exp).then_inc(s_exp, 1)

            def step(b, p, c):
                q = 1 - p
                l1 = exists(b)
                l0 = c is not None
                if l1:
                    act.wait_ge(s_conv1, b + 1)
                    wait(act, s_conv2, b)
                    act.activation(h_pad[:, HALO:HALO + N], bank[CHAN], ACT.Relu, bias=vec(SH1), scale=vec(SC1)).then_inc(s_h1, 1)
                    act.wait_ge(s_emb, b + 1)
                    wait(act, s_dist, 4 * b)
                    act.activation(emb_m[0:NSE, :], bank[CHAN][0:NSE, :], ACT.Identity, bias=se_bias[0:NSE, 0:1]).then_inc(s_emb_parts, 1)
                    act.activation(emb_n[0:NSE, :], bank[CHAN][0:NSE, :], ACT.Identity, bias=se_bias2[0:NSE, 0:1], scale=2.0).then_inc(s_emb_parts, 1)
                    act.activation(emb_n[32:32 + NSE, :], bank[CHAN][32:32 + NSE, :], ACT.Square, bias=se_bias[32:32 + NSE, 0:1]).then_inc(s_emb_parts, 1)
                    act.activation(emb_m[64:64 + NSE, :], bank[CHAN][64:64 + NSE, :], ACT.Square, bias=se_bias[64:64 + NSE, 0:1]).then_inc(s_emb_parts, 1)
                if l0:
                    adjt_even(c, q, 0)
                    adjt_even(c, q, 2)
                    act.wait_ge(s_turn[0], c + 1)
                    wait(act, s_t, c)
                    act.activation(xh0_t[:], bank[TURN_X], ACT.Copy, bias=1.0).then_inc(s_xt[0], 1)
                if l1:
                    for mt in range(NT):
                        exp(b, mt)
                if l0:
                    act.wait_ge(s_turn[1], c + 1)
                    wait(act, s_ffn, c)
                    act.activation(xh1_t[:], bank[TURN_X], ACT.Copy, bias=1.0).then_inc(s_xt[1], 1)
                if l1:
                    act.wait_ge(s_conv_pre, b + 1)
                    wait(act, s_z_ps, b)
                    act.activation(x_conv[:], conv_pre[:], ACT.Relu, bias=vec(SH2)).then_inc(s_x_conv, 1)
                    act.wait_ge(s_nmp, b + 1)
                    act.activation(x_nmp[:], bank[CHAN], ACT.Copy).then_inc(s_x_nmp, 1)
                    act.wait_ge(s_ghn_ps, b + 1)
                    wait(act, s_rh, b)
                    act.activation(gh_n[:], bank[TURN_B], ACT.Identity, bias=vec(HNB), scale=0.5).then_inc(s_gh_n, 1)
                if l0:
                    act.wait_ge(s_turn[2], c + 1)
                    if l1:
                        wait(act, s_x_less_n, b)
                        wait(act, s_z_ps, b)
                    act.activation(xc[q][:], bank[TURN_X], ACT.Copy).then_inc(s_xt[2], 1)
                if l1:
                    act.wait_ge(s_r_ps, b + 1)
                    act.activation(gate_r[:], bank[DIST_A], ACT.Tanh, bias=vec(RZB), scale=0.5).then_inc(s_r, 1)
                    act.wait_ge(s_z_ps, b + 1)
                    wait(act, s_z_part, b)
                    act.activation(gate_z[:], bank[DIST_B], ACT.Tanh, bias=vec(ZZB), scale=0.5).then_inc(s_z, 1)
                    act.wait_ge(s_n_pre, b + 1)
                    wait(act, s_upd, b)
                    act.activation(n_act[:], n_pre[:], ACT.Tanh, bias=vec(BN_)).then_inc(s_n, 1)

            steps(act, step)
            act.wait_ge(s_norm[3], B)

            def slot(it, k):
                before = earlier(it, k, LAG_S)
                if before is not None:
                    _, j, s = before
                    act.wait_ge(f_u, s + 1)
                    wait(act, f_norm, s - 3)
                    wait(act, f_norm_act, s - 3)
                    act.activation(g_ring[j % 4], u_ring[j % 2], ACT.Silu).then_inc(f_silu, 1)
                before = earlier(it, k, LAG_T)
                if before is not None:
                    _, j, s = before
                    act.wait_ge(f_turn, s + 1)
                    act.activation(y_all[:, GT * j:GT * j + GT, :].rearrange("p t c -> p (t c)"),
                                   g_ps[j % 2].rearrange("p h n -> p (h n)"), ACT.Copy).then_inc(f_state, 1)
                if not (isinstance(it, int) and it == ITERS):
                    if isinstance(it, int) and it == 0:
                        src = y_all[:, GT * k:GT * k + GT, :].rearrange("p t c -> p (t c)")
                    else:
                        act.wait_ge(f_mm, (it - 1) * GROUPS + k + 1)
                        src = y_ps[k % 2].rearrange("p h n -> p (h n)")
                    wait(act, f_u, it * GROUPS + k - 1)
                    act.activation(t_ring[k % 2], src, ACT.Tanh).then_inc(f_tanh, 1)
                before = earlier(it, k, LAG_A)
                if before is not None:
                    _, j, s = before
                    act.wait_ge(f_pow, s + 1)
                    wait(act, f_turn, s - 3)
                    for t in range(GT - ACT_TILES, GT):
                        ins = act.activation(tiles(h_ring[j % 4])[:, t, :], tiles(g_ring[j % 4])[:, t, :], ACT.Copy,
                                             scale=f_rs[:, j % 4, t:t + 1])
                    ins.then_inc(f_norm_act, 1)
            slots(act, slot)

        @block.vector
        def _(dve):
            count = [0]

            def link(ins):
                count[0] += 1
                ins.then_inc(s_fold, 1)
                dve.wait_ge(s_fold, count[0])

            def vec(c):
                return bcol[:, c:c + 1]

            dve.memset(half_neg[:], -0.5)
            dve.memset(ident[:], 1.0).then_inc(s_const, 1)
            dve.memset(ones_bf[:], 1.0)
            dve.memset(bias1[:], 0.0)
            dve.memset(b1_cols[:], 0.0)
            dve.memset(wse[:], 0.0)
            dve.memset(h_pad[:], 0.0)
            dve.memset(emb_m[:], 0.0)
            link(dve.memset(emb_n[:], 0.0))
            dve.memset(emb_m[32:32 + NSE, :], -1.0)
            dve.memset(emb_n[64:64 + NSE, :], -1.0)
            dve.wait_ge(s_small, 16 * NSMALL)
            dve.wait_ge(s_wload, 16 * NWEIGHTS)
            dve.wait_ge(s_pow, 2)
            for j, bc in ((0, B0), (1, BF)):
                link(dve.tensor_reduce(vec(T0), nat[:, j, :], AX_X, ALU.add))
                link(dve.tensor_tensor(vec(T1), vec(bc), vec(T0), ALU.subtract))
                link(dve.tensor_scalar(vec(T0), vec(T1), 1.0 / C, None, ALU.mult))
                link(dve.tensor_scalar(nat[:, j, :], nat[:, j, :], vec(T0), None, ALU.add))
            link(dve.tensor_tensor(tmp_w[:], nat[:, 2, :], lnb_row[:], ALU.mult))
            link(dve.tensor_reduce(vec(T0), tmp_w[:], AX_X, ALU.add))
            link(dve.tensor_tensor(vec(FB1), vec(T0), vec(B1), ALU.add))
            link(dve.tensor_tensor(nat[:, 2, :], nat[:, 2, :], lnw_row[:], ALU.mult))
            link(dve.tensor_reduce(vec(T0), nat[:, 2, :], AX_X, ALU.add))
            link(dve.tensor_scalar(vec(T1), vec(T0), -1.0 / C, None, ALU.mult))
            link(dve.tensor_scalar(nat[:, 2, :], nat[:, 2, :], vec(T1), float(C) ** 0.5, ALU.add, ALU.mult))
            for r in range(3):
                dve.tensor_copy(b1_cols[:, 32 * r:32 * r + 1], vec(FB1)).then_inc(s_brow if r == 2 else s_fold, 1)
                count[0] += r < 2
            dve.tensor_scalar(se_bias2[0:NSE, :], se_bias[0:NSE, :], 2.0, None, ALU.mult).then_inc(s_folded, 1)
            for g, be, m, sc, sh, t in ((G1, BE1, M1, SC1, SH1, T0), (G2, BE2, M2, SC2, SH2, T1)):
                link(dve.tensor_tensor(vec(sc), vec(sc), vec(g), ALU.mult))
                link(dve.tensor_tensor(vec(t), vec(m), vec(sc), ALU.mult))
                link(dve.tensor_tensor(vec(sh), vec(be), vec(t), ALU.subtract))
            for a, h, dst in ((BR, HR, RZB), (BZ, HZ, ZZB)):
                link(dve.tensor_tensor(vec(T0), vec(a), vec(h), ALU.add))
                link(dve.tensor_scalar(vec(dst), vec(T0), 0.5, None, ALU.mult))
            link(dve.tensor_scalar(vec(HNB), vec(HN), 0.5, None, ALU.mult))
            for j in range(8):
                dve.wait_ge(s_wturn, j + 1)
                if j < 7:
                    dve.tensor_copy(wt[:, 4 * j:4 * j + 4, :], tiles(bank[j])).then_inc(s_wcopy, 1)
                else:
                    dve.tensor_copy(wt[:, 28:31, :], tiles(bank[7])[:, 0:3, :])
                    for r in range(3):
                        last = dve.tensor_copy(wse[:, 32 * r:32 * r + NSE], bank[7][:, 3 * C:3 * C + NSE])
                    last.then_inc(s_wcopy, 1)
            dve.wait_ge(s_brow, 2)
            link(dve.tensor_copy(part_f[:, 0, :], psum[0:KD, 0, 0:C]))
            link(dve.tensor_copy(part_bf[:, 0, :], part_f[:, 0, :]))
            link(dve.tensor_tensor(part_f[:, 1, :], part_f[:, 0, :], part_bf[:, 0, :], ALU.subtract))
            link(dve.tensor_copy(part_bf[:, 1, :], part_f[:, 1, :]))
            link(dve.tensor_tensor(part_f[:, 2, :], part_f[:, 1, :], part_bf[:, 1, :], ALU.subtract))
            link(dve.tensor_copy(part_bf[:, 2, :], part_f[:, 2, :]))
            for t in range(NT):
                for r in range(3):
                    last = dve.tensor_copy(bias1[32 * r:32 * r + 1, t, :], part_bf[32 * r:32 * r + 1, r, :])
            last.then_inc(s_ready, 1)

            def x_graph(b):
                return x_tok[:, graph(b), :]

            def stats(w, n):
                settle(dve, s_passed_dve)
                for t in range(NT):
                    ins = dve.bn_stats(ln_stat[:, w, t, :], x_tok[:, bass.ds(n * NT + t, 1), :].rearrange("p t c -> p (t c)"))
                ins.then_inc(s_stat[w], 1)
                dve.wait_ge(s_stat[w], n + 1)
                settle(dve, s_passed_dve)
                for t in range(NT):
                    ins = dve.bn_aggr(ln_mv[:, w, t, :], ln_stat[:, w, t, :])
                ins.then_inc(s_mv[w], 1)

            def norm(w, n):
                dve.wait_ge(s_rs[w], 2 * n + 2)
                if w < 3:
                    wait(dve, s_turn[w], n)
                for t in range(NT):
                    dst = xh[:, w, t:t + 1, :] if w < 3 else y_all[:, bass.ds(n * NT + t, 1), :]
                    ins = dve.tensor_scalar(dst, x_tok[:, bass.ds(n * NT + t, 1), :], ln_mv[:, w, t, 0:1],
                                            ln_rs[:, w, t:t + 1], ALU.subtract, ALU.mult)
                ins.then_inc(s_norm[w], 1)

            def adjt_odd(c, q, mt):
                dve.wait_ge(s_adj_turned, 4 * c + mt + 1)
                wait(dve, s_edge_p, 2 * (c - 1))
                dve.tensor_copy(adj_t[q][:, mt, :], bank[TURN_B]).then_inc(s_adjt_odd, 1)

            def edges(b, p, mt):
                dve.wait_ge(s_exp, 4 * b + mt + 1)
                dve.tensor_tensor(edge[:, mt, :], edge[:, mt, :], adj_t[p][:, mt, :], ALU.mult).then_inc(s_edge_v, 1)

            def step(b, p, c):
                q = 1 - p
                l1 = exists(b)
                l0 = c is not None
                if l0:
                    dve.wait_ge(s_in[q], loaded(c, q))
                    stats(0, c)
                    wait(dve, s_dinv, 2 * c)
                    dve.tensor_reduce(deg[:], adj_in[q], AX_X, ALU.add).then_inc(s_deg, 1)
                    dve.wait_ge(s_deg, 3 * c + 1)
                    dve.tensor_scalar(deg0[:, 0, :], deg[:], 0.0, None, ALU.not_equal).then_inc(s_deg, 1)
                    dve.scalar_tensor_tensor(out=deg0[:, 1, :], in0=deg[:], scalar=0.0, in1=deg[:],
                                             op0=ALU.is_equal, op1=ALU.add).then_inc(s_deg, 1)
                    norm(0, c)
                if l1:
                    dve.wait_ge(s_msg, b + 1)
                    wait(dve, s_msg_tok, b)
                    dve.tensor_tensor(msg_pre[:], tiles(bank[TOK]),
                                      bmsg_row[:].rearrange("p (o c) -> p o c", o=1).broadcast_to([P, NT, C]),
                                      ALU.add).then_inc(s_msg_pre, 1)
                if l0:
                    adjt_odd(c, q, 1)
                if later(b):
                    dve.wait_ge(s_back, b)
                    dve.tensor_tensor(x_graph(b - 1), x_graph(b - 1), tiles(bank[TURN_X]), ALU.add).then_inc(s_x3, 1)
                if l0:
                    adjt_odd(c, q, 3)
                if later(b):
                    dve.wait_ge(s_x3, b)
                    stats(3, b - 1)
                if l0:
                    dve.wait_ge(s_t, c + 1)
                    dve.wait_ge(s_dinv, 2 * c + 2)
                    wait(dve, s_agg, c)
                    dve.tensor_tensor(t_tok[:], tiles(bank[TOK]), spread(dinv[:], NT, C), ALU.mult).then_inc(s_t_scaled, 1)
                if later(b):
                    norm(3, b - 1)
                if l1:
                    edges(b, p, 1)
                if l0:
                    dve.wait_ge(s_agg, c + 1)
                    dve.tensor_tensor(agg_tok[:], tiles(bank[TOK]), spread(dinv[:], NT, C), ALU.mult).then_inc(s_agg_scaled, 1)
                    dve.wait_ge(s_agg_scaled, c + 1)
                    dve.scalar_tensor_tensor(out=x_graph(c), in0=agg_tok[:], scalar=0.0, in1=x_graph(c),
                                             op0=ALU.max, op1=ALU.add).then_inc(s_x1, 1)
                    dve.wait_ge(s_x1, c + 1)
                    stats(1, c)
                if l1:
                    edges(b, p, 3)
                if l0:
                    norm(1, c)
                if l1:
                    dve.wait_ge(s_conv2, b + 1)
                    wait(dve, s_x_conv, b)
                    dve.scalar_tensor_tensor(out=conv_pre[:], in0=bank[CONV], scalar=vec(SC2), in1=xc[p][:],
                                             op0=ALU.mult, op1=ALU.add).then_inc(s_conv_pre, 1)
                if l0:
                    dve.wait_ge(s_ffn, c + 1)
                    dve.tensor_tensor(x_graph(c), x_graph(c), tiles(bank[TOK]), ALU.add).then_inc(s_x2, 1)
                    dve.wait_ge(s_x2, c + 1)
                    stats(2, c)
                    norm(2, c)
                if l1:
                    dve.wait_ge(s_r, b + 1)
                    dve.wait_ge(s_gh_n, b + 1)
                    dve.scalar_tensor_tensor(out=rh[:], in0=gate_r[:], scalar=1.0, in1=gh_n[:],
                                             op0=ALU.add, op1=ALU.mult).then_inc(s_rh, 1)
                    dve.wait_ge(s_rh, b + 1)
                    dve.wait_ge(s_gin_ps, b + 1)
                    wait(dve, s_n, b)
                    dve.tensor_tensor(n_pre[:], rh[:], bank[TURN_A], ALU.add).then_inc(s_n_pre, 1)
                    dve.wait_ge(s_n, b + 1)
                    dve.tensor_tensor(x_less_n[:], xc[p][:], n_act[:], ALU.subtract).then_inc(s_x_less_n, 1)
                    dve.wait_ge(s_x_less_n, b + 1)
                    dve.wait_ge(s_z, b + 1)
                    dve.scalar_tensor_tensor(out=z_part[:], in0=gate_z[:], scalar=1.0, in1=x_less_n[:],
                                             op0=ALU.add, op1=ALU.mult).then_inc(s_z_part, 1)
                    dve.wait_ge(s_z_part, b + 1)
                    wait(dve, s_back, b)
                    dve.scalar_tensor_tensor(out=upd[:], in0=z_part[:], scalar=0.5, in1=n_act[:],
                                             op0=ALU.mult, op1=ALU.add).then_inc(s_upd, 1)

            steps(dve, step)

            def slot(it, k):
                group = slice(GT * k, GT * k + GT)
                if isinstance(it, int) and it == ITERS:
                    dve.wait_ge(f_mm, (ITERS - 1) * GROUPS + k + 1)
                    dve.tensor_tensor(y_all[:, group, :], x_tok[:, group, :],
                                      y_ps[k % 2].rearrange("p h (t c) -> p (h t) c", c=C), ALU.add).then_inc(f_out, 1)
                else:
                    s = it * GROUPS + k
                    dve.wait_ge(f_tanh, s + 1)
                    wait(dve, f_silu, s - 1)
                    if isinstance(it, int) and it == 0:
                        src = y_all[:, group, :].rearrange("p t c -> p (t c)")
                    else:
                        src = y_ps[k % 2].rearrange("p h n -> p (h n)")
                    dve.scalar_tensor_tensor(out=u_ring[k % 2], in0=t_ring[k % 2], scalar=STEP, in1=src,
                                             op0=ALU.mult, op1=ALU.add).then_inc(f_u, 1)
                now, before = earlier(it, k, LAG_S), earlier(it, k, LAG_V)

                def bn(first, last):
                    if now is None:
                        return
                    _, j, s = now
                    if first == 0:
                        dve.wait_ge(f_silu, s + 1)
                        wait(dve, f_sm, s * 2 - 2)
                    for t in range(first, last):
                        ins = dve.bn_stats(f_stat[:, j % 2, t, :], g_ring[j % 4][:, C * t:C * t + C])
                    if last == GT:
                        ins.then_inc(f_bn, 1)

                bn(0, 2)
                if before is not None:
                    _, j, s = before
                    r = j % 2
                    dve.wait_ge(f_bn, s + 1)
                    dve.tensor_tensor(f_small[:, 0, :], f_stat[:, r, :, 1], f_stat[:, r, :, 4], ALU.subtract)
                    dve.scalar_tensor_tensor(out=f_small[:, 1, :], in0=f_stat[:, r, :, 2], scalar=C * EPS,
                                             in1=f_stat[:, r, :, 5], op0=ALU.add, op1=ALU.add).then_inc(f_sm, 1)
                bn(2, 4)
                if before is not None:
                    dve.wait_ge(f_sm, s * 2 + 1)
                    dve.scalar_tensor_tensor(out=f_small[:, 2, :], in0=f_small[:, 0, :], scalar=C / 4,
                                             in1=f_small[:, 0, :], op0=ALU.mult, op1=ALU.mult).then_inc(f_sm, 1)
                bn(4, 6)
                if before is not None:
                    dve.wait_ge(f_sm, s * 2 + 2)
                    wait(dve, f_pow, s - 1)
                    dve.tensor_tensor(f_var[:, r, :], f_small[:, 1, :], f_small[:, 2, :], ALU.add).then_inc(f_v, 1)
                bn(6, GT)

            slots(dve, slot)


_INS = ['x', 'adj', 'L0_gnn_W', 'L0_gnn_b', 'L0_ffn_weight', 'L0_ffn_bias', 'L1_gnn_w_se', 'L1_gnn_b_se',
        'L1_gnn_conv1_w', 'L1_gnn_bn1_g', 'L1_gnn_bn1_b', 'L1_gnn_bn1_m', 'L1_gnn_bn1_v', 'L1_gnn_conv2_w',
        'L1_gnn_bn2_g', 'L1_gnn_bn2_b', 'L1_gnn_bn2_m', 'L1_gnn_bn2_v', 'L1_gnn_w_msg', 'L1_gnn_b_msg',
        'L1_gnn_w_ih', 'L1_gnn_b_ih', 'L1_gnn_w_hh', 'L1_gnn_b_hh', 'L1_ffn_ln_w', 'L1_ffn_ln_b', 'L1_ffn_W',
        'L1_ffn_b']


def kernel(**inputs):
    import numpy as _np
    import concourse.bacc as _bacc
    from concourse import mybir as _mybir
    from concourse.bass_utils import run_bass_kernel_spmd as _run

    nc = _bacc.Bacc("TRN2", target_bir_lowering=False, num_devices=1)
    arrays, aps = {}, {}
    for name in _INS:
        a = _np.ascontiguousarray(inputs[name])
        arrays[f"in_{name}_dram"] = a
        aps[name] = nc.dram_tensor(f"in_{name}_dram", a.shape, _mybir.dt.from_np(a.dtype), kind="ExternalInput").ap()
    out = nc.dram_tensor("out_0_dram", inputs['x'].shape, _mybir.dt.float32, kind="ExternalOutput").ap()
    g = {k[len('L1_gnn_'):]: v for k, v in aps.items() if k.startswith('L1_gnn_')}
    build(nc, aps['x'], aps['adj'], aps['L0_gnn_W'], aps['L0_gnn_b'], aps['L0_ffn_weight'], aps['L0_ffn_bias'],
          g['w_se'], g['b_se'], g['conv1_w'], [g['bn1_g'], g['bn1_b'], g['bn1_m'], g['bn1_v']],
          g['conv2_w'], [g['bn2_g'], g['bn2_b'], g['bn2_m'], g['bn2_v']], g['w_msg'], g['b_msg'],
          g['w_ih'], g['b_ih'], g['w_hh'], g['b_hh'], aps['L1_ffn_ln_w'], aps['L1_ffn_ln_b'],
          aps['L1_ffn_W'], aps['L1_ffn_b'], out)
    r = _run(nc, [arrays], core_ids=[0])
    return r.results[0]["out_0_dram"]
```

```python
from contextlib import ExitStack

import concourse.bass as bass
from concourse import mybir

F32 = mybir.dt.float32
BF16 = mybir.dt.bfloat16
F32R = mybir.dt.float32r
ALU = mybir.AluOpType
ACT = mybir.ActivationFunctionType
AX_X = mybir.AxisListType.X

P = 128
B, N, C = 16, 512, 128
NT = N // P
TAPS = 17
HALO = TAPS // 2
EPS = 1e-5
ITERS = 30
STEP = 0.01
GT = 8
GROUPS = B * NT // GT
GN = GT * P
NSE = 3
QUAD = 32
KD = 3 * QUAD + 3 * NSE
KB = 2 * QUAD + 1
LAG_S = 2
LAG_V = 3
LAG_P = 4
LAG_A = 5
LAG_T = 7
ACT_TILES = 1


def wait(eng, sem, count):
    if not isinstance(count, int) or count > 0:
        eng.wait_ge(sem, count)


def settle(eng, passed):
    eng.sem_inc(passed, 1)


def tiles(ap):
    return ap.rearrange("p (t c) -> p t c", c=C)


def spread(col, n, width):
    return col.rearrange("p (t o) -> p t o", o=1).broadcast_to([P, n, width])


def build(nc, x, adj, w0, b0, wf, bf, w_se, b_se, conv1_w, bn1, conv2_w, bn2, w_msg, b_msg,
          w_ih, b_ih, w_hh, b_hh, ln_w, ln_b, w1, b1, out):
    with ExitStack() as ctx:
        def sb(name, shape, dt=F32):
            return ctx.enter_context(nc.sbuf_tensor(name, shape, dt))

        def sem(name):
            return ctx.enter_context(nc.semaphore(name))

        x_tok = sb("x_tok", [P, B * NT, C])
        y_all = sb("y_all", [P, B * NT, C])
        w1_t = sb("w1_t", [P, C])
        ident = sb("ident", [P, P])
        ones_bf = sb("ones_bf", [KB, P], BF16)
        bias1 = sb("bias1", [KB, NT, C], BF16)
        half_neg = sb("half_neg", [P, 8])

        phase_a = ctx.enter_context(ExitStack())

        def sba(name, shape, dt=F32):
            return phase_a.enter_context(nc.sbuf_tensor(name, shape, dt))

        def split(name, shape):
            return sba(name + "_h", shape, F32R), sba(name + "_l", shape, F32R)

        work = sba("work", [P, 20 * N])

        def piece(first, count):
            return work[:, first * N:(first + count) * N]

        adj_in = [piece(4 * p, 4).rearrange("p (t m) -> p t m", m=N) for p in range(2)]
        adj_t = [piece(8 + 4 * p, 4).rearrange("p (t n) -> p t n", n=N) for p in range(2)]
        edge = piece(16, 4).rearrange("p (t n) -> p t n", n=N)
        conv2_nat = work[:, 0:C * TAPS].rearrange("p (i k) -> p i k", k=TAPS)
        nat = tiles(piece(16, 4))

        spare = piece(8, 4)
        emb_row = spare[0:1, 0:8 * P].rearrange("o (j q i) -> o j q i", j=8, q=4)
        part_f = tiles(spare[0:KB, 8 * P:8 * P + 3 * C])
        lnw_row, lnb_row, tmp_w = (spare[:, 8 * P + (3 + j) * C:8 * P + (4 + j) * C] for j in range(3))
        b1_cols = spare[:, 8 * P + 6 * C:8 * P + 6 * C + KB]

        wt = split("wt", [P, 15 + TAPS, C])
        CONV2, W0, WF, W1 = 0, TAPS, TAPS + 1, TAPS + 2
        IH, HH, MSG, CONV1, WSE = TAPS + 3, TAPS + 9, TAPS + 12, TAPS + 13, TAPS + 14
        wse = split("wse", [P, 4, QUAD])
        part_bf = sba("part_bf", [KB, 3, C], BF16)
        bcol = sba("bcol", [P, 32])
        bmsg_row = sba("bmsg_row", [P, C])
        emb_vec = sba("emb_vec", [KD, 8])

        ln_stat = sba("ln_stat", [P, 4, NT, 6])
        ln_mv = sba("ln_mv", [P, 4, NT, 2])
        ln_ve = sba("ln_ve", [P, 4, NT])
        ln_rs = sba("ln_rs", [P, 4, NT])
        xh = sba("xh", [P, NT, C])
        xh_t = split("xh_t", [P, N])
        xc = [sba(f"xc{p}", [P, N]) for p in range(2)]
        xc_s = split("xc_s", [P, N])
        deg = sba("deg", [P, NT])
        deg0 = sba("deg0", [P, 3, NT])
        dinv = sba("dinv", [P, NT])
        t_tok = sba("t_tok", [P, NT, C])
        agg_tok = sba("agg_tok", [P, NT, C])
        h_full = sba("h_full", [P, N])
        h_pad = split("h_pad", [P, N + 2 * HALO])
        emb_m = sba("emb_m", [KD, N], F32R)
        emb_n = sba("emb_n", [KD, N], F32R)
        emb_f = [[sba(f"emb_f{w}{k}", [KD, N]) for k in range(2)] for w in range(2)]
        msg_pre = sba("msg_pre", [P, NT, C])
        msg_tok = sba("msg_tok", [P, NT, C])
        conv_pre = sba("conv_pre", [P, N])
        x_conv = split("x_conv", [P, N])
        x_nmp = split("x_nmp", [P, N])
        gate_r = sba("gate_r", [P, N])
        gate_z = sba("gate_z", [P, N])
        gh_n = sba("gh_n", [P, N])
        n_pre = sba("n_pre", [P, N])
        n_act = sba("n_act", [P, N])
        x_less_n = sba("x_less_n", [P, N])
        upd = sba("upd", [P, N])

        phase_a.close()
        t_ring = [sb(f"t_ring{r}", [P, GN])[:] for r in range(2)]
        u_ring = [sb(f"u_ring{r}", [P, GN])[:] for r in range(2)]
        g_ring = [sb(f"g_ring{r}", [P, GN])[:] for r in range(4)]
        h_ring = [sb(f"h_ring{r}", [P, GN])[:] for r in range(4)]
        f_stat = sb("f_stat", [P, 2, GT, 6])
        f_small = sb("f_small", [P, 3, GT])
        f_var = sb("f_var", [P, 2, GT])
        f_rs = sb("f_rs", [P, 4, GT])

        psum = ctx.enter_context(nc.psum_tensor("psum", [P, 8, N], F32))
        bank = [psum[:, i, :] for i in range(8)]
        TURN_A, TURN_B, TURN_X, TOK, CONV, CHAN, DIST_A, DIST_B = range(8)
        y_ps = [psum[:, 2 * r:2 * r + 2, :] for r in range(2)]
        g_ps = [psum[:, 4 + 2 * r:6 + 2 * r, :] for r in range(2)]

        s_small = sem("s_small")
        s_wload = sem("s_wload")
        s_const = sem("s_const")
        s_ident = sem("s_ident")
        s_fold = sem("s_fold")
        s_folded = sem("s_folded")
        s_pow = sem("s_pow")
        s_wturn = sem("s_wturn")
        s_wcopy = sem("s_wcopy")
        s_brow = sem("s_brow")
        s_ready = sem("s_ready")
        s_in = [sem(f"s_in{p}") for p in range(2)]
        s_adj_turned = sem("s_adj_turned")
        s_adjt_even = sem("s_adjt_even")
        s_adjt_odd = sem("s_adjt_odd")
        s_deg = sem("s_deg")
        s_dinv = sem("s_dinv")
        s_stat = [sem(f"s_stat{w}") for w in range(4)]
        s_mv = [sem(f"s_mv{w}") for w in range(4)]
        s_rs = [sem(f"s_rs{w}") for w in range(4)]
        s_norm = [sem(f"s_norm{w}") for w in range(4)]
        s_turn = [sem(f"s_turn{w}") for w in range(3)]
        s_xt = [sem(f"s_xt{w}") for w in range(3)]
        s_xl = [sem(f"s_xl{w}") for w in range(3)]
        s_t = sem("s_t")
        s_t_scaled = sem("s_t_scaled")
        s_agg = sem("s_agg")
        s_agg_scaled = sem("s_agg_scaled")
        s_x1 = sem("s_x1")
        s_ffn = sem("s_ffn")
        s_x2 = sem("s_x2")
        s_conv1 = sem("s_conv1")
        s_h1 = sem("s_h1")
        s_h1_lo = sem("s_h1_lo")
        s_emb = sem("s_emb")
        s_emb_sg = sem("s_emb_sg")
        s_emb_v = sem("s_emb_v")
        s_emb_hi = sem("s_emb_hi")
        s_emb_lo = sem("s_emb_lo")
        s_msg = sem("s_msg")
        s_msg_pre = sem("s_msg_pre")
        s_msg_tok = sem("s_msg_tok")
        s_conv2 = sem("s_conv2")
        s_conv_pre = sem("s_conv_pre")
        s_x_conv = sem("s_x_conv")
        s_x_conv_lo = sem("s_x_conv_lo")
        s_dist = sem("s_dist")
        s_exp = sem("s_exp")
        s_edge_p = sem("s_edge_p")
        s_edge_v = sem("s_edge_v")
        s_nmp = sem("s_nmp")
        s_x_nmp = sem("s_x_nmp")
        s_x_nmp_lo = sem("s_x_nmp_lo")
        s_embrow = sem("s_embrow")
        s_embvec = sem("s_embvec")
        s_ghn_ps = sem("s_ghn_ps")
        s_gh_n = sem("s_gh_n")
        s_r_ps = sem("s_r_ps")
        s_r = sem("s_r")
        s_z_ps = sem("s_z_ps")
        s_z = sem("s_z")
        s_gin_ps = sem("s_gin_ps")
        s_rh = sem("s_rh")
        s_n_pre = sem("s_n_pre")
        s_n = sem("s_n")
        s_x_less_n = sem("s_x_less_n")
        s_z_part = sem("s_z_part")
        s_upd = sem("s_upd")
        s_back = sem("s_back")
        s_x3 = sem("s_x3")
        f_mm = sem("f_mm")
        f_tanh = sem("f_tanh")
        f_u = sem("f_u")
        f_silu = sem("f_silu")
        f_bn = sem("f_bn")
        f_sm = sem("f_sm")
        f_v = sem("f_v")
        f_pow = sem("f_pow")
        f_norm = sem("f_norm")
        f_norm_act = sem("f_norm_act")
        f_turn = sem("f_turn")
        f_state = sem("f_state")
        f_out = sem("f_out")
        s_store = sem("s_store")
        s_passed_sp = sem("s_passed_sp")
        s_passed_pool = sem("s_passed_pool")
        s_passed_dve = sem("s_passed_dve")

        block = ctx.enter_context(nc.Block())

        def graph(b):
            return bass.ds(b * NT, NT)

        x_dram = x.rearrange("b (t p) c -> b p t c", p=P)
        adj_dram = adj.rearrange("b (t p) m -> b p t m", p=P)
        out_dram = out.rearrange("b (t p) c -> p (b t) c", p=P)

        def col(v):
            return v.rearrange("(p o) -> p o", o=1)

        (B0, BF, B1, G1, BE1, M1, V1, G2, BE2, M2, V2, BR, BZ, BN_, HR, HZ, HN,
         SC1, SH1, SC2, SH2, RZB, ZZB, HNB, T0, T1, FB1) = range(27)
        small = [(b0, B0), (bf, BF), (b1, B1)] + list(zip(bn1, (G1, BE1, M1, V1))) + \
            list(zip(bn2, (G2, BE2, M2, V2))) + \
            [(b_ih[C * j:C * j + C], BR + j) for j in range(3)] + [(b_hh[C * j:C * j + C], HR + j) for j in range(3)]
        EMB_BIAS = [(1, 0), (1, 2), (3, 2), (5, 0), (5, 1), (7, 1)]
        EMB_CONST = [(0, 0, 1.0), (0, 2, 1.0), (1, 1, -1.0), (2, 2, 1.0), (3, 0, 1.0), (3, 1, 1.0),
                     (4, 0, 2.0), (4, 1, 1.0), (5, 2, -1.0), (6, 1, 1.0), (7, 0, 1.0), (7, 2, 1.0)]
        NSMALL = len(small) + len(EMB_BIAS) + 3
        weights = [(conv2_nat, conv2_w), (nat[:, 0, :], w0), (nat[:, 1, :], wf), (nat[:, 2, :], w1)] + \
            [(nat[:, 3 + 2 * j:5 + 2 * j, :], w_ih[C * j:C * j + C, :].rearrange("o (h i) -> o h i", h=2)) for j in range(3)] + \
            [(nat[:, 9 + j, :], w_hh[C * j:C * j + C, :]) for j in range(3)] + \
            [(nat[:, 12, :], w_msg), (nat[:, 13, :], conv1_w.rearrange("o i k -> o (i k)")), (nat[0:NSE, 14, :], w_se)]
        NWEIGHTS = len(weights)

        def steps(eng, step):
            step(None, 0, None, 0)
            step(None, 1, 0, 1)
            for b in range(2):
                step(b, b % 2, b + 1, b + 2)
            with eng.Fori(1, B // 2 - 1) as i:
                for p in range(2):
                    step(i * 2 + p, p, i * 2 + (p + 1), i * 2 + (p + 2))
            step(B - 2, 0, B - 1, None)
            step(B - 1, 1, None, None)
            step(B, 0, None, None)

        def slots(eng, slot):
            for k in range(GROUPS):
                slot(0, k)
            with eng.Fori(1, ITERS) as it:
                for k in range(GROUPS):
                    slot(it, k)
            for k in range(GROUPS):
                slot(ITERS, k)

        def loaded(c, q):
            return (c + 2 - q) * 16

        def later(b):
            return b is not None and not (isinstance(b, int) and b == 0)

        def exists(b):
            return b is not None and not (isinstance(b, int) and b == B)

        def earlier(it, k, lag):
            if k >= lag:
                if isinstance(it, int) and it == ITERS:
                    return None
                return it, k - lag, it * GROUPS + (k - lag)
            if isinstance(it, int) and it == 0:
                return None
            return it - 1, k - lag + GROUPS, (it - 1) * GROUPS + (k - lag + GROUPS)

        @block.sync
        def _(sp):
            for dst, src in weights:
                sp.dma_start(dst, src).then_inc(s_wload, 16)
            sp.wait_ge(s_embrow, 1)
            for v, c in small:
                sp.dma_start(bcol[:, c:c + 1], col(v)).then_inc(s_small, 16)
            for j, t in EMB_BIAS:
                sp.dma_start(emb_row[:, j, :, NSE * t:NSE * t + NSE],
                             b_se.rearrange("(o q i) -> o q i", o=1, q=1).broadcast_to([1, 4, NSE])).then_inc(s_small, 16)
            for row, v in ((lnw_row, ln_w), (lnb_row, ln_b), (bmsg_row, b_msg)):
                sp.dma_start(row[:], v.rearrange("(o c) -> o c", o=1).broadcast_to([P, C])).then_inc(s_small, 16)

            def load(b, p):
                wait(sp, s_adj_turned, 4 * (b - 1))
                settle(sp, s_passed_sp)
                wait(sp, s_deg, 3 * (b - 1))
                settle(sp, s_passed_sp)
                sp.dma_start(adj_in[p], adj_dram[b]).then_inc(s_in[p], 16)
                sp.dma_start(x_tok[:, graph(b), :], x_dram[b]).then_inc(s_in[p], 16)

            sp.wait_ge(s_wturn, 5)
            load(0, 0)
            load(1, 1)
            with sp.Fori(1, B // 2) as i:
                for p in range(2):
                    load(i * 2 + p, p)
            for k in range(GROUPS):
                sp.wait_ge(f_out, k + 1)
                sp.dma_start(out_dram[:, GT * k:GT * k + GT, :], y_all[:, GT * k:GT * k + GT, :]).then_inc(s_store, 16)
            sp.wait_ge(s_store, 16 * GROUPS)

        @block.gpsimd
        def _(pool):
            pool.wait_ge(s_const, 1)
            pool.affine_select(out=ident[:], in_=ident[:], compare_op=ALU.is_equal, fill=0.0, base=0,
                               pattern=[[-1, P]], channel_multiplier=1).then_inc(s_ident, 1)
            pool.wait_ge(s_small, 16 * NSMALL)
            pool.tensor_scalar(bcol[:, T0:T0 + 1], bcol[:, V1:V1 + 1], 1.0, EPS, ALU.mult, ALU.add)
            pool.tensor_scalar(bcol[:, T1:T1 + 1], bcol[:, V2:V2 + 1], 1.0, EPS, ALU.mult, ALU.add).then_inc(s_pow, 1)
            pool.wait_ge(s_pow, 1)
            pool.tensor_tensor(bcol[:, SC1:SC1 + 1], bcol[:, T0:T0 + 1], half_neg[:, 0:1], ALU.pow)
            pool.tensor_tensor(bcol[:, SC2:SC2 + 1], bcol[:, T1:T1 + 1], half_neg[:, 0:1], ALU.pow).then_inc(s_pow, 1)

            def rstd(w, n):
                pool.wait_ge(s_mv[w], n + 1)
                settle(pool, s_passed_pool)
                pool.tensor_scalar(ln_ve[:, w, :], ln_mv[:, w, :, 1], 1.0, EPS, ALU.mult, ALU.add).then_inc(s_rs[w], 1)
                pool.wait_ge(s_rs[w], 2 * n + 1)
                pool.tensor_tensor(ln_rs[:, w, :], ln_ve[:, w, :], half_neg[:, 0:NT], ALU.pow).then_inc(s_rs[w], 1)

            def edges(b, p, mt):
                pool.wait_ge(s_exp, 4 * b + mt + 1)
                pool.tensor_tensor(edge[:, mt, :], edge[:, mt, :], adj_t[p][:, mt, :], ALU.mult).then_inc(s_edge_p, 1)

            def step(b, p, c, d):
                l1 = exists(b)
                if l1:
                    for w in range(2):
                        pool.wait_ge(s_emb_sg, 2 * b + w + 1)
                        pool.tensor_tensor(emb_f[w][0][:], emb_f[w][0][:], emb_f[w][1][:], ALU.mult).then_inc(s_emb_v, 1)
                    pool.wait_ge(s_msg_pre, b + 1)
                    wait(pool, s_nmp, b)
                    settle(pool, s_passed_pool)
                    pool.tensor_scalar(msg_tok[:], msg_pre[:], 0.0, None, ALU.max).then_inc(s_msg_tok, 1)
                if c is not None:
                    rstd(1, c)
                if l1:
                    edges(b, p, 0)
                if later(b):
                    rstd(3, b - 1)
                if l1:
                    edges(b, p, 2)
                if c is not None:
                    rstd(2, c)
                if l1:
                    pool.wait_ge(s_x_conv, 2 * b + 2)
                    wait(pool, s_z_ps, b)
                    pool.tensor_tensor(x_conv[1][:], conv_pre[:], x_conv[0][:].bitcast(F32), ALU.subtract).then_inc(s_x_conv_lo, 1)
                if d is not None:
                    rstd(0, d)
                    pool.wait_ge(s_deg, 3 * d + 3)
                    wait(pool, s_x1, d)
                    pool.tensor_tensor(deg0[:, 2, :], deg0[:, 1, :], half_neg[:, 0:NT], ALU.pow).then_inc(s_dinv, 1)
                    pool.wait_ge(s_dinv, 2 * d + 1)
                    pool.tensor_tensor(dinv[:], deg0[:, 2, :], deg0[:, 0, :], ALU.mult).then_inc(s_dinv, 1)

            steps(pool, step)

            def slot(it, k):
                before = earlier(it, k, LAG_P)
                if before is None:
                    return
                _, j, s = before
                pool.wait_ge(f_v, s + 1)
                wait(pool, f_norm_act, s - 3)
                pool.tensor_tensor(f_rs[:, j % 4, :], f_var[:, j % 2, :], half_neg[:, 0:GT], ALU.pow).then_inc(f_pow, 1)
                pool.wait_ge(f_pow, s + 1)
                wait(pool, f_turn, s - 3)
                t = GT - ACT_TILES
                pool.tensor_tensor(tiles(h_ring[j % 4])[:, 0:t, :], tiles(g_ring[j % 4])[:, 0:t, :],
                                   spread(f_rs[:, j % 4, 0:t], t, C), ALU.mult).then_inc(f_norm, 1)

            slots(pool, slot)

        @block.tensor
        def _(pe):
            pe.wait_ge(s_ident, 1)
            pe.wait_ge(s_folded, 1)
            pe.wait_ge(s_wload, 16 * NWEIGHTS)
            for j in range(TAPS + 15):
                if j < TAPS:
                    src, rows = conv2_nat[:, :, j], P
                elif j == WSE:
                    src, rows = nat[0:NSE, j - TAPS, :], NSE
                else:
                    src, rows = nat[:, j - TAPS, :], P
                m = pe.transpose(psum[:, j // 4, C * (j % 4):C * (j % 4) + rows], src, ident[0:rows, 0:rows])
                if j % 4 == 3:
                    m.then_inc(s_wturn, 1)
            pe.wait_ge(s_wcopy, 8)
            pe.wait_ge(s_brow, 1)
            pe.matmul(psum[0:KB, 0, 0:C], b1_cols[:], ident[:], start=True, stop=True).then_inc(s_brow, 1)
            pe.wait_ge(s_embrow, 2)
            for j in range(8):
                m = pe.matmul(psum[0:KD, 1, 2 * j:2 * j + 1], emb_row[:, j, :, :].rearrange("o q i -> o (q i)")[:, 0:KD],
                              ident[0:1, 0:1], start=True, stop=True)
            m.then_inc(s_embvec, 1)
            pe.wait_ge(s_ready, 1)

            def w(j):
                return wt[0][:, j, :], wt[1][:, j, :]

            def product(dst, lhs, rhs, start=True, stop=True):
                pe.matmul(dst, lhs[0], rhs[0], start=start, stop=False)
                pe.matmul(dst, lhs[0], rhs[1], start=False, stop=False)
                return pe.matmul(dst, lhs[1], rhs[0], start=False, stop=stop)

            def cut(parts, first, count):
                return parts[0][:, first:first + count], parts[1][:, first:first + count]

            def turn(k, n):
                pe.wait_ge(s_norm[k], n + 1)
                for t in range(NT):
                    m = pe.transpose(bank[TURN_X][:, P * t:P * t + P], xh[:, t, :], ident[:])
                m.then_inc(s_turn[k], 1)

            def tokens(dst, lhs, rhs, done):
                for t in range(NT):
                    m = product(dst[:, C * t:C * t + C], cut(lhs, P * t, P), rhs)
                m.then_inc(done, 1)

            def adj_turn(d, p, mt):
                if mt >= 2:
                    pe.wait_ge(s_adjt_even if mt == 2 else s_adjt_odd, 2 * d + 1)
                bk = bank[TURN_A if mt % 2 == 0 else TURN_B]
                for t in range(NT):
                    m = pe.transpose(bk[:, P * t:P * t + P], adj_in[p][:, t, P * mt:P * mt + P], ident[:])
                m.then_inc(s_adj_turned, 1)

            def step(b, p, c, d):
                q = 1 - p
                l1 = exists(b)
                l0 = c is not None

                def conv2(first, last):
                    if not l1:
                        return
                    if first == 0:
                        pe.wait_ge(s_h1_lo, b + 1)
                        wait(pe, s_conv_pre, b)
                    for k in range(first, last):
                        m = product(bank[CONV], w(CONV2 + k), cut(h_pad, k, N), start=(k == 0), stop=(k == TAPS - 1))
                    if last == TAPS:
                        m.then_inc(s_conv2, 1)

                def dist(mt):
                    if not l1:
                        return
                    if mt == 0:
                        pe.wait_ge(s_emb_lo, b + 1)
                        wait(pe, s_r, b)
                    if mt == 1:
                        wait(pe, s_z, b)
                    if mt >= 2:
                        pe.wait_ge(s_exp, 4 * b + mt - 1)
                    pe.matmul(bank[DIST_A + mt % 2], emb_m[:, P * mt:P * mt + P], emb_n[:],
                              start=True, stop=True).then_inc(s_dist, 1)

                if l1:
                    pe.wait_ge(s_xt[2], b + 1)
                    pe.wait_ge(s_xl[2], b + 1)
                    wait(pe, s_x_nmp_lo, b)
                    product(bank[CHAN], w(CONV1), cut(xc_s, 0, N)).then_inc(s_conv1, 1)
                    pe.wait_ge(s_x2, b + 1)
                    tokens(bank[TOK], xc_s, w(MSG), s_msg)
                if l0:
                    pe.wait_ge(s_xt[0], c + 1)
                    pe.wait_ge(s_xl[0], c + 1)
                    pe.wait_ge(s_adjt_odd, 2 * c + 2)
                    if b is not None:
                        wait(pe, s_gh_n, b)
                    tokens(bank[TURN_B], xh_t, w(W0), s_t)
                if l1:
                    pe.wait_ge(s_h1, b + 1)
                    product(bank[CHAN][0:KD, :], [x[:].rearrange("p q i -> p (q i)")[:, 0:KD] for x in wse],
                            cut(xc_s, 0, N)).then_inc(s_emb, 1)
                conv2(0, 3)
                if l0:
                    pe.wait_ge(s_t_scaled, c + 1)
                    pe.wait_ge(s_adjt_even, 2 * c + 2)
                    if l1:
                        pe.wait_ge(s_msg_pre, b + 1)
                    for t in range(NT):
                        for mt in range(NT):
                            m = pe.matmul(bank[TOK][:, C * t:C * t + C], adj_t[q][:, mt, P * t:P * t + P],
                                          t_tok[:, mt, :], start=(mt == 0), stop=(mt == NT - 1))
                    m.then_inc(s_agg, 1)
                conv2(3, 7)
                if later(b):
                    pe.wait_ge(s_upd, b)
                    if not l1:
                        pe.wait_ge(s_x3, b - 1)
                    for t in range(NT):
                        m = pe.transpose(bank[TURN_X][:, C * t:C * t + C], upd[:, P * t:P * t + P], ident[:])
                    m.then_inc(s_back, 1)
                dist(0)
                dist(1)
                conv2(7, 11)
                if l0:
                    if later(b):
                        pe.wait_ge(s_x3, b)
                    turn(1, c)
                dist(2)
                dist(3)
                conv2(11, 14)
                if l0:
                    pe.wait_ge(s_xt[1], c + 1)
                    pe.wait_ge(s_xl[1], c + 1)
                    pe.wait_ge(s_agg_scaled, c + 1)
                    tokens(bank[TOK], xh_t, w(WF), s_ffn)
                conv2(14, TAPS)
                if d is not None:
                    pe.wait_ge(s_in[p], loaded(d, p))
                    if later(b):
                        pe.wait_ge(s_n_pre, b)
                    adj_turn(d, p, 0)
                    adj_turn(d, p, 1)
                if l1:
                    pe.wait_ge(s_msg_tok, b + 1)
                    for mt in range(NT):
                        if mt % 2 == 0:
                            pe.wait_ge(s_edge_p, 2 * b + mt // 2 + 1)
                        else:
                            pe.wait_ge(s_edge_v, 2 * b + mt // 2 + 1)
                        m = pe.matmul(bank[CHAN], msg_tok[:, mt, :], edge[:, mt, :], start=(mt == 0), stop=(mt == NT - 1))
                    m.then_inc(s_nmp, 1)
                if d is not None:
                    adj_turn(d, p, 2)
                    adj_turn(d, p, 3)
                if l1:
                    x_in = cut(xc_s, 0, N)
                    pe.wait_ge(s_exp, 4 * b + 4)
                    product(bank[DIST_A], w(HH), x_in, stop=False)
                    product(bank[DIST_B], w(HH + 1), x_in, stop=False)
                    if d is not None:
                        pe.wait_ge(s_adjt_odd, 2 * d + 2)
                    elif not l0:
                        pe.wait_ge(s_gh_n, b)
                    product(bank[TURN_B], w(HH + 2), x_in).then_inc(s_ghn_ps, 1)
                if l0:
                    turn(2, c)
                if l1:
                    x_c, x_n = cut(x_conv, 0, N), cut(x_nmp, 0, N)
                    pe.wait_ge(s_x_conv, 2 * b + 1)
                    pe.wait_ge(s_x_conv_lo, b + 1)
                    product(bank[DIST_A], w(IH), x_c, start=False, stop=False)
                    product(bank[DIST_B], w(IH + 2), x_c, start=False, stop=False)
                    pe.wait_ge(s_x_nmp, b + 1)
                    pe.wait_ge(s_x_nmp_lo, b + 1)
                    product(bank[DIST_A], w(IH + 1), x_n, start=False).then_inc(s_r_ps, 1)
                    if d is not None:
                        pe.wait_ge(s_adjt_even, 2 * d + 2)
                    else:
                        pe.wait_ge(s_n_pre, b)
                    product(bank[TURN_A], w(IH + 4), x_c, stop=False)
                    product(bank[TURN_A], w(IH + 5), x_n, start=False).then_inc(s_gin_ps, 1)
                if d is not None:
                    if l0:
                        pe.wait_ge(s_xl[2], c + 1)
                    turn(0, d)
                if l1:
                    product(bank[DIST_B], w(IH + 3), x_n, start=False).then_inc(s_z_ps, 1)

            steps(pe, step)

            def slot(it, k):
                before = earlier(it, k, LAG_T)
                if before is not None:
                    _, j, s = before
                    pe.wait_ge(f_norm, s + 1)
                    pe.wait_ge(f_norm_act, s + 1)
                    wait(pe, f_state, s - 1)
                    for t in range(GT):
                        m = pe.transpose(g_ps[j % 2][:, t // NT, P * (t % NT):P * (t % NT) + P],
                                         tiles(h_ring[j % 4])[:, t, :], ident[:])
                    m.then_inc(f_turn, 1)
                if not (isinstance(it, int) and it == 0):
                    s = (it - 1) * GROUPS + k
                    pe.wait_ge(f_state, s + 1)
                    if isinstance(it, int) and it == ITERS:
                        if k >= 2:
                            pe.wait_ge(f_out, k - 1)
                        else:
                            pe.wait_ge(f_u, ITERS * GROUPS - 1 + k)
                    else:
                        pe.wait_ge(f_u, s + GROUPS - 1)
                    for h in range(2):
                        pe.matmul(y_ps[k % 2][:, h, :], ones_bf[:], bias1[:].rearrange("p t c -> p (t c)"),
                                  start=True, stop=False, skip_group_check=True)
                        for t in range(NT):
                            m = pe.matmul(y_ps[k % 2][:, h, C * t:C * t + C], y_all[:, GT * k + NT * h + t, :], w1_t[:],
                                          start=False, stop=True, skip_group_check=True)
                    m.then_inc(f_mm, 1)

            slots(pe, slot)


        @block.scalar
        def _(act):
            act.wait_ge(s_ready, 1)

            def vec(c):
                return bcol[:, c:c + 1]

            def adjt_even(c, q, mt):
                act.wait_ge(s_adj_turned, 4 * c + mt + 1)
                wait(act, s_edge_p, 2 * (c - 1))
                wait(act, s_edge_v, 2 * (c - 1))
                act.activation(adj_t[q][:, mt, :], bank[TURN_A], ACT.Copy).then_inc(s_adjt_even, 1)

            def exp(b, mt):
                act.wait_ge(s_dist, 4 * b + mt + 1)
                wait(act, s_nmp, b)
                act.activation(edge[:, mt, :], bank[DIST_A + mt % 2], ACT.Exp).then_inc(s_exp, 1)

            def step(b, p, c, d):
                q = 1 - p
                l1 = exists(b)
                l0 = c is not None
                if l1:
                    act.wait_ge(s_conv1, b + 1)
                    wait(act, s_conv2, b)
                    act.activation(h_full[:], bank[CHAN], ACT.Relu, bias=vec(SH1), scale=vec(SC1))
                    act.activation(h_pad[0][:, HALO:HALO + N], bank[CHAN], ACT.Relu, bias=vec(SH1), scale=vec(SC1)).then_inc(s_h1, 1)
                    act.wait_ge(s_emb, b + 1)
                    wait(act, s_emb_lo, b)
                    for m in range(2):
                        for k in range(2):
                            j = 4 * m + 2 * k
                            ins = act.activation(emb_f[m][k][:], bank[CHAN][0:KD, :], ACT.Identity,
                                                 bias=emb_vec[:, j + 1:j + 2], scale=emb_vec[:, j:j + 1])
                        ins.then_inc(s_emb_sg, 1)
                if later(b):
                    act.wait_ge(s_n_pre, b)
                    wait(act, s_upd, b - 1)
                    act.activation(n_act[:], n_pre[:], ACT.Tanh, bias=vec(BN_)).then_inc(s_n, 1)
                if l1:
                    wait(act, s_dist, 4 * b)
                    for m, emb in enumerate((emb_m, emb_n)):
                        act.wait_ge(s_emb_v, 2 * b + m + 1)
                        act.activation(emb[:], emb_f[m][0][:], ACT.Copy).then_inc(s_emb_hi, 1)
                    for mt in range(NT):
                        exp(b, mt)
                if l0:
                    act.wait_ge(s_turn[1], c + 1)
                    act.wait_ge(s_t, c + 1)
                    act.activation(xh_t[0][:], bank[TURN_X], ACT.Copy, bias=1.0).then_inc(s_xt[1], 1)
                if l1:
                    act.wait_ge(s_conv_pre, b + 1)
                    wait(act, s_z_ps, b)
                    act.activation(x_conv[0][:], conv_pre[:], ACT.Relu, bias=vec(SH2)).then_inc(s_x_conv, 1)
                    act.wait_ge(s_x_conv, 2 * b + 1)
                    act.activation(conv_pre[:], conv_pre[:], ACT.Relu, bias=vec(SH2)).then_inc(s_x_conv, 1)
                if d is not None:
                    adjt_even(d, p, 0)
                if l1:
                    act.wait_ge(s_nmp, b + 1)
                    act.activation(x_nmp[0][:], bank[CHAN], ACT.Copy).then_inc(s_x_nmp, 1)
                if d is not None:
                    adjt_even(d, p, 2)
                if l1:
                    act.wait_ge(s_ghn_ps, b + 1)
                    wait(act, s_rh, b)
                    act.activation(gh_n[:], bank[TURN_B], ACT.Identity, bias=vec(HNB), scale=0.5).then_inc(s_gh_n, 1)
                if l0:
                    act.wait_ge(s_turn[2], c + 1)
                    if later(b):
                        act.wait_ge(s_x_less_n, b)
                    act.activation(xc_s[0][:], bank[TURN_X], ACT.Copy)
                    act.activation(xc[q][:], bank[TURN_X], ACT.Copy).then_inc(s_xt[2], 1)
                if l1:
                    act.wait_ge(s_r_ps, b + 1)
                    act.activation(gate_r[:], bank[DIST_A], ACT.Tanh, bias=vec(RZB), scale=0.5).then_inc(s_r, 1)
                if d is not None:
                    act.wait_ge(s_turn[0], d + 1)
                    wait(act, s_ffn, d)
                    act.activation(xh_t[0][:], bank[TURN_X], ACT.Copy, bias=1.0).then_inc(s_xt[0], 1)
                if l1:
                    act.wait_ge(s_z_ps, b + 1)
                    wait(act, s_z_part, b)
                    act.activation(gate_z[:], bank[DIST_B], ACT.Tanh, bias=vec(ZZB), scale=0.5).then_inc(s_z, 1)

            steps(act, step)
            act.wait_ge(s_norm[3], B)

            def slot(it, k):
                before = earlier(it, k, LAG_S)
                if before is not None:
                    _, j, s = before
                    act.wait_ge(f_u, s + 1)
                    wait(act, f_norm, s - 3)
                    wait(act, f_norm_act, s - 3)
                    act.activation(g_ring[j % 4], u_ring[j % 2], ACT.Silu).then_inc(f_silu, 1)
                before = earlier(it, k, LAG_T)
                if before is not None:
                    _, j, s = before
                    act.wait_ge(f_turn, s + 1)
                    act.activation(y_all[:, GT * j:GT * j + GT, :].rearrange("p t c -> p (t c)"),
                                   g_ps[j % 2].rearrange("p h n -> p (h n)"), ACT.Copy).then_inc(f_state, 1)
                if not (isinstance(it, int) and it == ITERS):
                    if isinstance(it, int) and it == 0:
                        src = y_all[:, GT * k:GT * k + GT, :].rearrange("p t c -> p (t c)")
                    else:
                        act.wait_ge(f_mm, (it - 1) * GROUPS + k + 1)
                        src = y_ps[k % 2].rearrange("p h n -> p (h n)")
                    wait(act, f_u, it * GROUPS + k - 1)
                    act.activation(t_ring[k % 2], src, ACT.Tanh).then_inc(f_tanh, 1)
                before = earlier(it, k, LAG_A)
                if before is not None:
                    _, j, s = before
                    act.wait_ge(f_pow, s + 1)
                    wait(act, f_turn, s - 3)
                    for t in range(GT - ACT_TILES, GT):
                        ins = act.activation(tiles(h_ring[j % 4])[:, t, :], tiles(g_ring[j % 4])[:, t, :], ACT.Copy,
                                             scale=f_rs[:, j % 4, t:t + 1])
                    ins.then_inc(f_norm_act, 1)
            slots(act, slot)

        @block.vector
        def _(dve):
            count = [0]

            def link(ins):
                count[0] += 1
                ins.then_inc(s_fold, 1)
                dve.wait_ge(s_fold, count[0])

            def vec(c):
                return bcol[:, c:c + 1]

            dve.memset(half_neg[:], -0.5)
            dve.memset(ident[:], 1.0).then_inc(s_const, 1)
            dve.memset(ones_bf[:], 1.0)
            dve.memset(bias1[:], 0.0)
            dve.memset(b1_cols[:], 0.0)
            for k in range(2):
                dve.memset(wse[k][:].bitcast(F32), 0.0)
                dve.memset(h_pad[k][:].bitcast(F32), 0.0)
            link(dve.memset(emb_row[:], 0.0))
            for j, t, value in EMB_CONST:
                ins = dve.memset(emb_row[:, j, :, NSE * t:NSE * t + NSE], value)
            ins.then_inc(s_embrow, 1)
            dve.wait_ge(s_small, 16 * NSMALL)
            dve.wait_ge(s_wload, 16 * NWEIGHTS)
            dve.wait_ge(s_pow, 2)
            for j, bc in ((0, B0), (1, BF)):
                link(dve.tensor_reduce(vec(T0), nat[:, j, :], AX_X, ALU.add))
                link(dve.tensor_tensor(vec(T1), vec(bc), vec(T0), ALU.subtract))
                link(dve.tensor_scalar(vec(T0), vec(T1), 1.0 / C, None, ALU.mult))
                link(dve.tensor_scalar(nat[:, j, :], nat[:, j, :], vec(T0), None, ALU.add))
            link(dve.tensor_tensor(tmp_w[:], nat[:, 2, :], lnb_row[:], ALU.mult))
            link(dve.tensor_reduce(vec(T0), tmp_w[:], AX_X, ALU.add))
            link(dve.tensor_tensor(vec(FB1), vec(T0), vec(B1), ALU.add))
            link(dve.tensor_tensor(nat[:, 2, :], nat[:, 2, :], lnw_row[:], ALU.mult))
            link(dve.tensor_reduce(vec(T0), nat[:, 2, :], AX_X, ALU.add))
            link(dve.tensor_scalar(vec(T1), vec(T0), -1.0 / C, None, ALU.mult))
            link(dve.tensor_scalar(nat[:, 2, :], nat[:, 2, :], vec(T1), float(C) ** 0.5, ALU.add, ALU.mult))
            for r in range(3):
                dve.tensor_copy(b1_cols[:, 32 * r:32 * r + 1], vec(FB1)).then_inc(s_brow if r == 2 else s_fold, 1)
                count[0] += r < 2
            dve.tensor_scalar(emb_row[:, 5, :, 0:NSE], emb_row[:, 5, :, 0:NSE], 2.0, None, ALU.mult).then_inc(s_embrow, 1)
            dve.wait_ge(s_embrow, 2)
            dve.sem_inc(s_folded, 1)
            for g, be, m, sc, sh, t in ((G1, BE1, M1, SC1, SH1, T0), (G2, BE2, M2, SC2, SH2, T1)):
                link(dve.tensor_tensor(vec(sc), vec(sc), vec(g), ALU.mult))
                link(dve.tensor_tensor(vec(t), vec(m), vec(sc), ALU.mult))
                link(dve.tensor_tensor(vec(sh), vec(be), vec(t), ALU.subtract))
            for a, h, dst in ((BR, HR, RZB), (BZ, HZ, ZZB)):
                link(dve.tensor_tensor(vec(T0), vec(a), vec(h), ALU.add))
                link(dve.tensor_scalar(vec(dst), vec(T0), 0.5, None, ALU.mult))
            link(dve.tensor_scalar(vec(HNB), vec(HN), 0.5, None, ALU.mult))
            for j in range(8):
                dve.wait_ge(s_wturn, j + 1)
                n = 4 if j < 7 else 3
                here = [wt[k][:, 4 * j:4 * j + n, :] for k in range(2)]
                link(dve.tensor_copy(here[0], tiles(bank[j])[:, 0:n, :]))
                ins = dve.tensor_tensor(here[1], tiles(bank[j])[:, 0:n, :], here[0].bitcast(F32), ALU.subtract)
                if j < 7:
                    ins.then_inc(s_wcopy, 1)
                if W1 // 4 == j:
                    dve.tensor_copy(w1_t[:], bank[j][:, C * (W1 % 4):C * (W1 % 4) + C])
            se = bank[7][:, 3 * C:3 * C + NSE].rearrange("p (q t i) -> p q t i", q=1, t=1).broadcast_to([P, 4, 3, NSE])
            here = [wse[k][:, :, 0:3 * NSE].rearrange("p q (t i) -> p q t i", i=NSE) for k in range(2)]
            link(dve.tensor_copy(here[0], se))
            dve.tensor_tensor(here[1], se, here[0].bitcast(F32), ALU.subtract).then_inc(s_wcopy, 1)
            dve.wait_ge(s_brow, 2)
            link(dve.tensor_copy(part_f[:, 0, :], psum[0:KB, 0, 0:C]))
            dve.wait_ge(s_embvec, 1)
            dve.tensor_copy(emb_vec[:], psum[0:KD, 1, 0:16].rearrange("p (j o) -> p j o", o=2)[:, :, 0])
            link(dve.tensor_copy(part_bf[:, 0, :], part_f[:, 0, :]))
            link(dve.tensor_tensor(part_f[:, 1, :], part_f[:, 0, :], part_bf[:, 0, :], ALU.subtract))
            link(dve.tensor_copy(part_bf[:, 1, :], part_f[:, 1, :]))
            link(dve.tensor_tensor(part_f[:, 2, :], part_f[:, 1, :], part_bf[:, 1, :], ALU.subtract))
            link(dve.tensor_copy(part_bf[:, 2, :], part_f[:, 2, :]))
            for t in range(NT):
                for r in range(3):
                    last = dve.tensor_copy(bias1[32 * r:32 * r + 1, t, :], part_bf[32 * r:32 * r + 1, r, :])
            last.then_inc(s_ready, 1)

            def x_graph(b):
                return x_tok[:, graph(b), :]

            def stats(w, n):
                settle(dve, s_passed_dve)
                for t in range(NT):
                    ins = dve.bn_stats(ln_stat[:, w, t, :], x_tok[:, bass.ds(n * NT + t, 1), :].rearrange("p t c -> p (t c)"))
                ins.then_inc(s_stat[w], 1)
                dve.wait_ge(s_stat[w], n + 1)
                settle(dve, s_passed_dve)
                for t in range(NT):
                    ins = dve.bn_aggr(ln_mv[:, w, t, :], ln_stat[:, w, t, :])
                ins.then_inc(s_mv[w], 1)

            def norm(w, n):
                dve.wait_ge(s_rs[w], 2 * n + 2)
                if w == 0:
                    wait(dve, s_turn[2], n)
                elif w < 3:
                    dve.wait_ge(s_turn[w - 1], n + 1)
                for t in range(NT):
                    dst = xh[:, t:t + 1, :] if w < 3 else y_all[:, bass.ds(n * NT + t, 1), :]
                    ins = dve.tensor_scalar(dst, x_tok[:, bass.ds(n * NT + t, 1), :], ln_mv[:, w, t, 0:1],
                                            ln_rs[:, w, t:t + 1], ALU.subtract, ALU.mult)
                ins.then_inc(s_norm[w], 1)

            def adjt_odd(c, q, mt):
                dve.wait_ge(s_adj_turned, 4 * c + mt + 1)
                wait(dve, s_edge_p, 2 * (c - 1))
                dve.tensor_copy(adj_t[q][:, mt, :], bank[TURN_B]).then_inc(s_adjt_odd, 1)

            def low(w, n):
                dve.wait_ge(s_xt[w], n + 1)
                dst, high = (xh_t if w < 2 else xc_s)[1], (xh_t if w < 2 else xc_s)[0][:].bitcast(F32)
                if w < 2:
                    ins = dve.scalar_tensor_tensor(out=dst[:], in0=bank[TURN_X], scalar=1.0, in1=high,
                                                   op0=ALU.add, op1=ALU.subtract)
                else:
                    ins = dve.tensor_tensor(dst[:], bank[TURN_X], high, ALU.subtract)
                ins.then_inc(s_xl[w], 1)

            def edges(b, p, mt):
                dve.wait_ge(s_exp, 4 * b + mt + 1)
                dve.tensor_tensor(edge[:, mt, :], edge[:, mt, :], adj_t[p][:, mt, :], ALU.mult).then_inc(s_edge_v, 1)

            def step(b, p, c, d):
                q = 1 - p
                l1 = exists(b)
                l0 = c is not None
                if l1:
                    dve.wait_ge(s_h1, b + 1)
                    wait(dve, s_conv2, b)
                    dve.tensor_tensor(h_pad[1][:, HALO:HALO + N], h_full[:], h_pad[0][:, HALO:HALO + N].bitcast(F32),
                                      ALU.subtract).then_inc(s_h1_lo, 1)
                if l0:
                    dve.wait_ge(s_t, c + 1)
                    dve.wait_ge(s_dinv, 2 * c + 2)
                    wait(dve, s_agg, c)
                    dve.tensor_tensor(t_tok[:], tiles(bank[TURN_B]), spread(dinv[:], NT, C), ALU.mult).then_inc(s_t_scaled, 1)
                if l1:
                    dve.wait_ge(s_msg, b + 1)
                    wait(dve, s_msg_tok, b)
                    dve.tensor_tensor(msg_pre[:], tiles(bank[TOK]),
                                      bmsg_row[:].rearrange("p (o c) -> p o c", o=1).broadcast_to([P, NT, C]),
                                      ALU.add).then_inc(s_msg_pre, 1)
                if later(b):
                    dve.wait_ge(s_r, b)
                    dve.wait_ge(s_gh_n, b)
                    wait(dve, s_n, b - 1)
                    dve.scalar_tensor_tensor(out=n_pre[:], in0=gate_r[:], scalar=1.0, in1=gh_n[:],
                                             op0=ALU.add, op1=ALU.mult).then_inc(s_rh, 1)
                    dve.wait_ge(s_rh, b)
                    dve.wait_ge(s_gin_ps, b)
                    dve.tensor_tensor(n_pre[:], n_pre[:], bank[TURN_A], ALU.add).then_inc(s_n_pre, 1)
                    dve.wait_ge(s_n, b)
                    dve.tensor_tensor(x_less_n[:], xc[q][:], n_act[:], ALU.subtract).then_inc(s_x_less_n, 1)
                    dve.wait_ge(s_x_less_n, b)
                    dve.wait_ge(s_z, b)
                    dve.scalar_tensor_tensor(out=x_less_n[:], in0=gate_z[:], scalar=1.0, in1=x_less_n[:],
                                             op0=ALU.add, op1=ALU.mult).then_inc(s_z_part, 1)
                    dve.wait_ge(s_z_part, b)
                    wait(dve, s_back, b - 1)
                    dve.scalar_tensor_tensor(out=upd[:], in0=x_less_n[:], scalar=0.5, in1=n_act[:],
                                             op0=ALU.mult, op1=ALU.add).then_inc(s_upd, 1)
                if l1:
                    dve.wait_ge(s_emb_hi, 2 * b + 2)
                    for m, emb, first, last in ((0, emb_m, 2, 4), (1, emb_n, 1, 2), (1, emb_n, 3, 4)):
                        rows = slice(QUAD * first, min(QUAD * last, KD))
                        ins = dve.tensor_tensor(emb[rows, :], emb_f[m][0][rows, :], emb[rows, :].bitcast(F32), ALU.subtract)
                    ins.then_inc(s_emb_lo, 1)
                if l0:
                    dve.wait_ge(s_agg, c + 1)
                    dve.tensor_tensor(agg_tok[:], tiles(bank[TOK]), spread(dinv[:], NT, C), ALU.mult).then_inc(s_agg_scaled, 1)
                    dve.wait_ge(s_agg_scaled, c + 1)
                    dve.scalar_tensor_tensor(out=x_graph(c), in0=agg_tok[:], scalar=0.0, in1=x_graph(c),
                                             op0=ALU.max, op1=ALU.add).then_inc(s_x1, 1)
                    dve.wait_ge(s_x1, c + 1)
                    stats(1, c)
                if later(b):
                    dve.wait_ge(s_back, b)
                    dve.tensor_tensor(x_graph(b - 1), x_graph(b - 1), tiles(bank[TURN_X]), ALU.add).then_inc(s_x3, 1)
                if l0:
                    norm(1, c)
                if l1:
                    edges(b, p, 1)
                if later(b):
                    dve.wait_ge(s_x3, b)
                    stats(3, b - 1)
                if l0:
                    low(1, c)
                if l1:
                    edges(b, p, 3)
                if later(b):
                    norm(3, b - 1)
                if l0:
                    dve.wait_ge(s_ffn, c + 1)
                    dve.tensor_tensor(x_graph(c), x_graph(c), tiles(bank[TOK]), ALU.add).then_inc(s_x2, 1)
                    dve.wait_ge(s_x2, c + 1)
                    stats(2, c)
                if l1:
                    dve.wait_ge(s_conv2, b + 1)
                    wait(dve, s_x_conv_lo, b)
                    dve.scalar_tensor_tensor(out=conv_pre[:], in0=bank[CONV], scalar=vec(SC2), in1=xc[p][:],
                                             op0=ALU.mult, op1=ALU.add).then_inc(s_conv_pre, 1)
                if l0:
                    norm(2, c)
                if d is not None:
                    dve.wait_ge(s_in[p], loaded(d, p))
                    stats(0, d)
                    adjt_odd(d, p, 1)
                    wait(dve, s_dinv, 2 * d)
                    dve.tensor_reduce(deg[:], adj_in[p], AX_X, ALU.add).then_inc(s_deg, 1)
                    dve.wait_ge(s_deg, 3 * d + 1)
                    dve.tensor_scalar(deg0[:, 0, :], deg[:], 0.0, None, ALU.not_equal).then_inc(s_deg, 1)
                    dve.scalar_tensor_tensor(out=deg0[:, 1, :], in0=deg[:], scalar=0.0, in1=deg[:],
                                             op0=ALU.is_equal, op1=ALU.add).then_inc(s_deg, 1)
                if l1:
                    dve.wait_ge(s_x_nmp, b + 1)
                    wait(dve, s_z_ps, b)
                    dve.tensor_tensor(x_nmp[1][:], bank[CHAN], x_nmp[0][:].bitcast(F32), ALU.subtract).then_inc(s_x_nmp_lo, 1)
                if d is not None:
                    adjt_odd(d, p, 3)
                if l0:
                    low(2, c)
                if d is not None:
                    norm(0, d)
                    low(0, d)

            steps(dve, step)

            def slot(it, k):
                group = slice(GT * k, GT * k + GT)
                if isinstance(it, int) and it == ITERS:
                    dve.wait_ge(f_mm, (ITERS - 1) * GROUPS + k + 1)
                    dve.tensor_tensor(y_all[:, group, :], x_tok[:, group, :],
                                      y_ps[k % 2].rearrange("p h (t c) -> p (h t) c", c=C), ALU.add).then_inc(f_out, 1)
                else:
                    s = it * GROUPS + k
                    dve.wait_ge(f_tanh, s + 1)
                    wait(dve, f_silu, s - 1)
                    if isinstance(it, int) and it == 0:
                        src = y_all[:, group, :].rearrange("p t c -> p (t c)")
                    else:
                        src = y_ps[k % 2].rearrange("p h n -> p (h n)")
                    dve.scalar_tensor_tensor(out=u_ring[k % 2], in0=t_ring[k % 2], scalar=STEP, in1=src,
                                             op0=ALU.mult, op1=ALU.add).then_inc(f_u, 1)
                now, before = earlier(it, k, LAG_S), earlier(it, k, LAG_V)

                def bn(first, last):
                    if now is None:
                        return
                    _, j, s = now
                    if first == 0:
                        dve.wait_ge(f_silu, s + 1)
                        wait(dve, f_sm, s * 2 - 2)
                    for t in range(first, last):
                        ins = dve.bn_stats(f_stat[:, j % 2, t, :], g_ring[j % 4][:, C * t:C * t + C])
                    if last == GT:
                        ins.then_inc(f_bn, 1)

                bn(0, 2)
                if before is not None:
                    _, j, s = before
                    r = j % 2
                    dve.wait_ge(f_bn, s + 1)
                    dve.tensor_tensor(f_small[:, 0, :], f_stat[:, r, :, 1], f_stat[:, r, :, 4], ALU.subtract)
                    dve.scalar_tensor_tensor(out=f_small[:, 1, :], in0=f_stat[:, r, :, 2], scalar=C * EPS,
                                             in1=f_stat[:, r, :, 5], op0=ALU.add, op1=ALU.add).then_inc(f_sm, 1)
                bn(2, 4)
                if before is not None:
                    dve.wait_ge(f_sm, s * 2 + 1)
                    dve.scalar_tensor_tensor(out=f_small[:, 2, :], in0=f_small[:, 0, :], scalar=C / 4,
                                             in1=f_small[:, 0, :], op0=ALU.mult, op1=ALU.mult).then_inc(f_sm, 1)
                bn(4, 6)
                if before is not None:
                    dve.wait_ge(f_sm, s * 2 + 2)
                    wait(dve, f_pow, s - 1)
                    dve.tensor_tensor(f_var[:, r, :], f_small[:, 1, :], f_small[:, 2, :], ALU.add).then_inc(f_v, 1)
                bn(6, GT)

            slots(dve, slot)


_INS = ['x', 'adj', 'L0_gnn_W', 'L0_gnn_b', 'L0_ffn_weight', 'L0_ffn_bias', 'L1_gnn_w_se', 'L1_gnn_b_se',
        'L1_gnn_conv1_w', 'L1_gnn_bn1_g', 'L1_gnn_bn1_b', 'L1_gnn_bn1_m', 'L1_gnn_bn1_v', 'L1_gnn_conv2_w',
        'L1_gnn_bn2_g', 'L1_gnn_bn2_b', 'L1_gnn_bn2_m', 'L1_gnn_bn2_v', 'L1_gnn_w_msg', 'L1_gnn_b_msg',
        'L1_gnn_w_ih', 'L1_gnn_b_ih', 'L1_gnn_w_hh', 'L1_gnn_b_hh', 'L1_ffn_ln_w', 'L1_ffn_ln_b', 'L1_ffn_W',
        'L1_ffn_b']


def kernel(**inputs):
    import numpy as _np
    import concourse.bacc as _bacc
    from concourse import mybir as _mybir
    from concourse.bass_utils import run_bass_kernel_spmd as _run

    nc = _bacc.Bacc("TRN2", target_bir_lowering=False, num_devices=1)
    arrays, aps = {}, {}
    for name in _INS:
        a = _np.ascontiguousarray(inputs[name])
        arrays[f"in_{name}_dram"] = a
        aps[name] = nc.dram_tensor(f"in_{name}_dram", a.shape, _mybir.dt.from_np(a.dtype), kind="ExternalInput").ap()
    out = nc.dram_tensor("out_0_dram", inputs['x'].shape, _mybir.dt.float32, kind="ExternalOutput").ap()
    g = {k[len('L1_gnn_'):]: v for k, v in aps.items() if k.startswith('L1_gnn_')}
    build(nc, aps['x'], aps['adj'], aps['L0_gnn_W'], aps['L0_gnn_b'], aps['L0_ffn_weight'], aps['L0_ffn_bias'],
          g['w_se'], g['b_se'], g['conv1_w'], [g['bn1_g'], g['bn1_b'], g['bn1_m'], g['bn1_v']],
          g['conv2_w'], [g['bn2_g'], g['bn2_b'], g['bn2_m'], g['bn2_v']], g['w_msg'], g['b_msg'],
          g['w_ih'], g['b_ih'], g['w_hh'], g['b_hh'], aps['L1_ffn_ln_w'], aps['L1_ffn_ln_b'],
          aps['L1_ffn_W'], aps['L1_ffn_b'], out)
    r = _run(nc, [arrays], core_ids=[0])
    return r.results[0]["out_0_dram"]
```

```python
from contextlib import ExitStack

import concourse.bass as bass
from concourse import mybir

F32 = mybir.dt.float32
BF16 = mybir.dt.bfloat16
F32R = mybir.dt.float32r
ALU = mybir.AluOpType
ACT = mybir.ActivationFunctionType
AX_X = mybir.AxisListType.X

P = 128
B, N, C = 16, 512, 128
NT = N // P
TAPS = 17
HALO = TAPS // 2
EPS = 1e-5
ITERS = 30
STEP = 0.01
GT = 8
GROUPS = B * NT // GT
GN = GT * P
NSE = 3
QUAD = 32
KD = 3 * QUAD + 3 * NSE
KB = 2 * QUAD + 1
LAG_S = 2
LAG_V = 3
LAG_P = 4
LAG_A = 5
LAG_T = 7
ACT_TILES = (2, 1, 1, 2, 1, 1, 2, 1)
DVE_TILES = (0, 1, 0, 0, 1, 0, 0, 1)
EARLY = 6


def wait(eng, sem, count):
    if not isinstance(count, int) or count > 0:
        eng.wait_ge(sem, count)


def settle(eng, passed):
    eng.sem_inc(passed, 1)


def tiles(ap):
    return ap.rearrange("p (t c) -> p t c", c=C)


def spread(col, n, width):
    return col.rearrange("p (t o) -> p t o", o=1).broadcast_to([P, n, width])


def build(nc, x, adj, w0, b0, wf, bf, w_se, b_se, conv1_w, bn1, conv2_w, bn2, w_msg, b_msg,
          w_ih, b_ih, w_hh, b_hh, ln_w, ln_b, w1, b1, out):
    with ExitStack() as ctx:
        def sb(name, shape, dt=F32):
            return ctx.enter_context(nc.sbuf_tensor(name, shape, dt))

        def sem(name):
            return ctx.enter_context(nc.semaphore(name))

        x_tok = sb("x_tok", [P, B * NT, C])
        y_all = sb("y_all", [P, B * NT, C])
        w1_t = sb("w1_t", [P, C])
        ident = sb("ident", [P, P])
        ones_bf = sb("ones_bf", [KB, P], BF16)
        bias1 = sb("bias1", [KB, NT, C], BF16)
        half_neg = sb("half_neg", [P, 8])
        f_stat = sb("f_stat", [P, 2, GT, 6])
        f_small = sb("f_small", [P, 3, GT])
        f_var = sb("f_var", [P, 2, GT])
        f_rs = sb("f_rs", [P, 4, GT])

        phase_a = ctx.enter_context(ExitStack())

        def sba(name, shape, dt=F32):
            return phase_a.enter_context(nc.sbuf_tensor(name, shape, dt))

        def split(name, shape):
            return sba(name + "_h", shape, F32R), sba(name + "_l", shape, F32R)

        work = sba("work", [P, 20 * N])

        def piece(first, count):
            return work[:, first * N:(first + count) * N]

        adj_in = [piece(4 * p, 4).rearrange("p (t m) -> p t m", m=N) for p in range(2)]
        adj_t = [piece(8 + 4 * p, 4).rearrange("p (t n) -> p t n", n=N) for p in range(2)]
        edge = piece(16, 4).rearrange("p (t n) -> p t n", n=N)
        conv2_nat = work[:, 12 * N:12 * N + C * TAPS].rearrange("p (i k) -> p i k", k=TAPS)
        nat = tiles(work[:, 12 * N + C * TAPS:20 * N])
        N_W0, N_WF, N_W1, N_MSG, N_IH, N_HH, N_CONV1, N_SE = 0, 1, 2, 3, 4, 10, 13, 14

        CONV2, IH, HH, CONV1 = 0, TAPS, TAPS + 6, TAPS + 9
        NSPLIT = TAPS + 10
        wt = split("wt", [P, NSPLIT, C])
        W0, WF, MSG = range(3)
        w_full = sba("w_full", [P, 3, C])
        wse = split("wse", [P, 4, QUAD])

        gates = sba("gates", [P, 4 * N])
        gate_r, gate_z, gh_n, n_pre = (gates[:, N * j:N * j + N] for j in range(4))
        emb_row = gates[0:1, 0:8 * P].rearrange("o (j q i) -> o j q i", j=8, q=4)
        part_f = tiles(gates[0:KB, 8 * P:8 * P + 3 * C])
        lnw_row, lnb_row, tmp_w = (gates[:, 8 * P + (3 + j) * C:8 * P + (4 + j) * C] for j in range(3))
        b1_cols = gates[:, 8 * P + 6 * C:8 * P + 6 * C + KB]
        emb_bias = gates[0:1, 8 * P + 7 * C:8 * P + 7 * C + NSE]

        part_bf = sba("part_bf", [KB, 3, C], BF16)
        bcol = sba("bcol", [P, 32])
        bmsg_row = sba("bmsg_row", [P, C])
        emb_vec = sba("emb_vec", [KD, 8])

        ln_stat = sba("ln_stat", [P, 4, NT, 6])
        ln_mv = sba("ln_mv", [P, 4, NT, 2])
        ln_ve = sba("ln_ve", [P, 4, NT])
        ln_rs = sba("ln_rs", [P, 4, NT])
        xh = sba("xh", [P, NT, C])
        xh_t = sba("xh_t", [P, N])
        xc = [sba(f"xc{p}", [P, N]) for p in range(2)]
        xc_s = split("xc_s", [P, N])
        deg = sba("deg", [P, NT])
        deg0 = sba("deg0", [P, 3, NT])
        dinv = sba("dinv", [P, NT])
        xs = sba("xs", [P, NT, C])
        agg_tok = sba("agg_tok", [P, NT, C])
        h_full = sba("h_full", [P, N])
        h_pad = split("h_pad", [P, N + 2 * HALO])
        emb_m = sba("emb_m", [KD, N], F32R)
        emb_n = sba("emb_n", [KD, N], F32R)
        emb_f = [[sba(f"emb_f{w}{k}", [KD, N]) for k in range(2)] for w in range(2)]
        msg_pre = sba("msg_pre", [P, NT, C])
        msg_tok = sba("msg_tok", [P, NT, C])
        conv_pre = sba("conv_pre", [P, N])
        x_conv = split("x_conv", [P, N])
        x_nmp = split("x_nmp", [P, N])
        n_act = sba("n_act", [P, N])
        x_less_n = sba("x_less_n", [P, N])
        upd = sba("upd", [P, N])

        phase_a.close()
        t_ring = [sb(f"t_ring{r}", [P, GN])[:] for r in range(2)]
        u_ring = [sb(f"u_ring{r}", [P, GN])[:] for r in range(2)]
        g_ring = [sb(f"g_ring{r}", [P, GN])[:] for r in range(4)]
        h_ring = [sb(f"h_ring{r}", [P, GN])[:] for r in range(4)]
        g_ring += [sb(f"g_ring{r}", [P, GN])[:] for r in range(4, GROUPS)]

        psum = ctx.enter_context(nc.psum_tensor("psum", [P, 8, N], F32))
        bank = [psum[:, i, :] for i in range(8)]
        TURN_A, TURN_B, TURN_X, TOK, CONV, CHAN, DIST_A, DIST_B = range(8)
        y_ps = [psum[:, 2 * r:2 * r + 2, :] for r in range(2)]
        g_ps = [psum[:, 4 + 2 * r:6 + 2 * r, :] for r in range(2)]

        s_first = sem("s_first")
        s_small = sem("s_small")
        s_wload = sem("s_wload")
        s_const = sem("s_const")
        s_ident = sem("s_ident")
        s_fold = sem("s_fold")
        s_folded0 = sem("s_folded0")
        s_folded1 = sem("s_folded1")
        s_chain = sem("s_chain")
        s_vectors = sem("s_vectors")
        s_wturn0 = sem("s_wturn0")
        s_wfull = sem("s_wfull")
        s_wturn = sem("s_wturn")
        s_whigh = sem("s_whigh")
        s_wlow = sem("s_wlow")
        s_rows = sem("s_rows")
        s_rows_read = sem("s_rows_read")
        s_ready = sem("s_ready")
        s_in = [sem(f"s_in{p}") for p in range(2)]
        s_adj_turned = sem("s_adj_turned")
        s_adjt_even = sem("s_adjt_even")
        s_adjt_odd = sem("s_adjt_odd")
        s_deg = sem("s_deg")
        s_dinv = sem("s_dinv")
        s_stat = [sem(f"s_stat{w}") for w in range(4)]
        s_mv = [sem(f"s_mv{w}") for w in range(4)]
        s_rs = [sem(f"s_rs{w}") for w in range(4)]
        s_norm = [sem(f"s_norm{w}") for w in range(4)]
        s_turn = {w: sem(f"s_turn{w}") for w in (1, 2)}
        s_xt = [sem(f"s_xt{w}") for w in range(3)]
        s_xl = sem("s_xl")
        s_xc = sem("s_xc")
        s_q = sem("s_q")
        s_xs = sem("s_xs")
        s_agg = sem("s_agg")
        s_agg_scaled = sem("s_agg_scaled")
        s_x1 = sem("s_x1")
        s_ffn = sem("s_ffn")
        s_x2 = sem("s_x2")
        s_conv1 = sem("s_conv1")
        s_h1 = sem("s_h1")
        s_h1_lo = sem("s_h1_lo")
        s_emb = sem("s_emb")
        s_emb_sg = sem("s_emb_sg")
        s_emb_v = sem("s_emb_v")
        s_emb_hi = sem("s_emb_hi")
        s_emb_lo = sem("s_emb_lo")
        s_msg = sem("s_msg")
        s_msg_pre = sem("s_msg_pre")
        s_msg_tok = sem("s_msg_tok")
        s_conv2 = sem("s_conv2")
        s_conv_pre = sem("s_conv_pre")
        s_x_conv = sem("s_x_conv")
        s_x_conv_lo = sem("s_x_conv_lo")
        s_dist = sem("s_dist")
        s_exp = sem("s_exp")
        s_edge_p = sem("s_edge_p")
        s_edge_v = sem("s_edge_v")
        s_nmp = sem("s_nmp")
        s_x_nmp = sem("s_x_nmp")
        s_x_nmp_lo = sem("s_x_nmp_lo")
        s_ghn_ps = sem("s_ghn_ps")
        s_gh_n = sem("s_gh_n")
        s_r_ps = sem("s_r_ps")
        s_r = sem("s_r")
        s_z_ps = sem("s_z_ps")
        s_z = sem("s_z")
        s_gin_ps = sem("s_gin_ps")
        s_rh = sem("s_rh")
        s_n_pre = sem("s_n_pre")
        s_n = sem("s_n")
        s_x_less_n = sem("s_x_less_n")
        s_z_part = sem("s_z_part")
        s_upd = sem("s_upd")
        s_back = sem("s_back")
        s_x3 = sem("s_x3")
        f_mm = sem("f_mm")
        f_tanh = sem("f_tanh")
        f_u = sem("f_u")
        f_silu = sem("f_silu")
        f_bn = sem("f_bn")
        f_sm = sem("f_sm")
        f_v = sem("f_v")
        f_pow = sem("f_pow")
        f_norm = sem("f_norm")
        f_norm_act = sem("f_norm_act")
        f_norm_dve = sem("f_norm_dve")
        f_turn = sem("f_turn")
        f_state = sem("f_state")
        f_out = sem("f_out")
        s_store = sem("s_store")
        s_passed_sp = sem("s_passed_sp")
        s_passed_pool = sem("s_passed_pool")
        s_passed_dve = sem("s_passed_dve")

        block = ctx.enter_context(nc.Block())

        def graph(b):
            return bass.ds(b * NT, NT)

        x_dram = x.rearrange("b (t p) c -> b p t c", p=P)
        adj_dram = adj.rearrange("b (t p) m -> b p t m", p=P)
        out_dram = out.rearrange("b (t p) c -> p (b t) c", p=P)

        def col(v):
            return v.rearrange("(p o) -> p o", o=1)

        (G1, G2, BE1, BE2, M1, M2, V1, V2, BR, BZ, BN_, HR, HZ, HN, SC1, SC2, SH1, SH2, RZB, ZZB, HNB,
         T0, T1, B0, BF, B1, FB1, S0, S1, U0, U1) = range(31)
        small = list(zip(bn1, (G1, BE1, M1, V1))) + list(zip(bn2, (G2, BE2, M2, V2))) + [(b1, B1)] + \
            [(b_ih[C * j:C * j + C], BR + j) for j in range(3)] + [(b_hh[C * j:C * j + C], HR + j) for j in range(3)]
        EMB_BIAS = [(1, 0, 1.0), (1, 2, 1.0), (3, 2, 1.0), (5, 0, 2.0), (5, 1, 1.0), (7, 1, 1.0)]
        EMB_CONST = [(0, 0, 1.0), (0, 2, 1.0), (1, 1, -1.0), (2, 2, 1.0), (3, 0, 1.0), (3, 1, 1.0),
                     (4, 0, 2.0), (4, 1, 1.0), (5, 2, -1.0), (6, 1, 1.0), (7, 0, 1.0), (7, 2, 1.0)]
        NSMALL = len(small) + 4
        weights = [(nat[:, N_W1, :], w1), (conv2_nat, conv2_w),
                   (nat[:, N_IH:N_IH + 6, :].rearrange("p (j h) i -> p j h i", h=2),
                    w_ih.rearrange("(j o) (h i) -> o j h i", o=C, h=2)),
                   (nat[:, N_HH:N_HH + 3, :], w_hh.rearrange("(j o) i -> o j i", o=C)),
                   (nat[:, N_MSG, :], w_msg), (nat[:, N_CONV1, :], conv1_w.rearrange("o i k -> o (i k)")),
                   (nat[0:NSE, N_SE, :], w_se)]
        NWEIGHTS = len(weights)
        FILLS = 8

        def embedding():
            at = 3 * C
            return bank[CONV + (FILLS - 2) % 4][:, at:at + NSE].rearrange("p (q t i) -> p q t i", q=1, t=1) \
                .broadcast_to([P, 4, 3, NSE])

        def parts_se(k):
            return wse[k][:, :, 0:3 * NSE].rearrange("p q (t i) -> p q t i", i=NSE)

        def steps(eng, step):
            step(None, 0, None, 0)
            step(None, 1, 0, 1)
            for b in range(2):
                step(b, b % 2, b + 1, b + 2)
            with eng.Fori(1, B // 2 - 1) as i:
                for p in range(2):
                    step(i * 2 + p, p, i * 2 + (p + 1), i * 2 + (p + 2))
            step(B - 2, 0, B - 1, None)
            step(B - 1, 1, None, None)
            step(B, 0, None, None)

        def slots(eng, slot):
            for k in range(EARLY, GROUPS):
                slot(0, k)
            with eng.Fori(1, ITERS) as it:
                for k in range(GROUPS):
                    slot(it, k)
            for k in range(GROUPS):
                slot(ITERS, k)

        def loaded(c, q):
            return (c + 2 - q) * 16

        def later(b):
            return b is not None and not (isinstance(b, int) and b == 0)

        def exists(b):
            return b is not None and not (isinstance(b, int) and b == B)

        def dve_norms(it, j):
            return it * sum(n > 0 for n in DVE_TILES) + sum(n > 0 for n in DVE_TILES[:j])

        def ends(b, last):
            return isinstance(b, int) and b == last

        def earlier(it, k, lag):
            if k >= lag:
                if isinstance(it, int) and it == ITERS:
                    return None
                return it, k - lag, it * GROUPS + (k - lag)
            if isinstance(it, int) and it == 0:
                return None
            return it - 1, k - lag + GROUPS, (it - 1) * GROUPS + (k - lag + GROUPS)

        @block.sync
        def _(sp):
            def load(b, p):
                wait(sp, s_adj_turned, 4 * (b - 1))
                settle(sp, s_passed_sp)
                wait(sp, s_deg, 3 * (b - 1))
                settle(sp, s_passed_sp)
                sp.dma_start(adj_in[p], adj_dram[b]).then_inc(s_in[p], 16)
                sp.dma_start(x_tok[:, graph(b), :], x_dram[b]).then_inc(s_in[p], 16)

            load(0, 0)
            for dst, src in ((nat[:, N_W0, :], w0), (nat[:, N_WF, :], wf),
                             (bcol[:, B0:B0 + 1], col(b0)), (bcol[:, BF:BF + 1], col(bf))):
                sp.dma_start(dst, src).then_inc(s_first, 16)
            for dst, src in weights:
                sp.dma_start(dst, src).then_inc(s_wload, 16)
            for row, v in ((lnw_row, ln_w), (lnb_row, ln_b), (bmsg_row, b_msg)):
                sp.dma_start(row[:], v.rearrange("(o c) -> o c", o=1).broadcast_to([P, C])).then_inc(s_small, 16)
            for v, c in small:
                sp.dma_start(bcol[:, c:c + 1], col(v)).then_inc(s_small, 16)
            sp.dma_start(emb_bias, b_se.rearrange("(o i) -> o i", o=1)).then_inc(s_small, 16)
            load(1, 1)
            with sp.Fori(1, B // 2) as i:
                for p in range(2):
                    load(i * 2 + p, p)
            for k in range(GROUPS):
                sp.wait_ge(f_out, k + 1)
                sp.dma_start(out_dram[:, GT * k:GT * k + GT, :], y_all[:, GT * k:GT * k + GT, :]).then_inc(s_store, 16)
            sp.wait_ge(s_store, 16 * GROUPS)

        @block.gpsimd
        def _(pool):
            pool.wait_ge(s_const, 1)
            pool.affine_select(out=ident[:], in_=ident[:], compare_op=ALU.is_equal, fill=0.0, base=0,
                               pattern=[[-1, P]], channel_multiplier=1).then_inc(s_ident, 1)

            def vectors():
                def pair(c):
                    return bcol[:, c:c + 2]

                count = [0]

                def link(ins):
                    count[0] += 1
                    ins.then_inc(s_chain, 1)
                    pool.wait_ge(s_chain, count[0])

                pool.wait_ge(s_small, 16 * NSMALL)
                link(pool.tensor_scalar(pair(T0), pair(V1), 1.0, EPS, ALU.mult, ALU.add))
                link(pool.tensor_tensor(pair(S0), pair(T0), half_neg[:, 0:2], ALU.pow))
                link(pool.tensor_tensor(pair(SC1), pair(S0), pair(G1), ALU.mult))
                link(pool.tensor_tensor(pair(U0), pair(M1), pair(SC1), ALU.mult))
                pool.tensor_tensor(pair(SH1), pair(BE1), pair(U0), ALU.subtract)
                link(pool.tensor_tensor(pair(S0), pair(BR), pair(HR), ALU.add))
                pool.tensor_scalar(pair(RZB), pair(S0), 0.5, None, ALU.mult)
                pool.tensor_scalar(bcol[:, HNB:HNB + 1], bcol[:, HN:HN + 1], 0.5, None, ALU.mult).then_inc(s_vectors, 1)

            def rstd(w, n):
                pool.wait_ge(s_mv[w], n + 1)
                settle(pool, s_passed_pool)
                pool.tensor_scalar(ln_ve[:, w, :], ln_mv[:, w, :, 1], 1.0, EPS, ALU.mult, ALU.add).then_inc(s_rs[w], 1)
                pool.wait_ge(s_rs[w], 2 * n + 1)
                pool.tensor_tensor(ln_rs[:, w, :], ln_ve[:, w, :], half_neg[:, 0:NT], ALU.pow).then_inc(s_rs[w], 1)

            def edges(b, p, mt):
                pool.wait_ge(s_exp, 4 * b + mt + 1)
                pool.tensor_tensor(edge[:, mt, :], edge[:, mt, :], adj_t[p][:, mt, :], ALU.mult).then_inc(s_edge_p, 1)

            def slot(it, k):
                before = earlier(it, k, LAG_P)
                if before is None:
                    return
                _, j, s = before
                pool.wait_ge(f_v, s + 1)
                wait(pool, f_norm_act, s - 3)
                pool.tensor_tensor(f_rs[:, j % 4, :], f_var[:, j % 2, :], half_neg[:, 0:GT], ALU.pow).then_inc(f_pow, 1)
                pool.wait_ge(f_pow, s + 1)
                wait(pool, f_turn, s - 3)
                t = GT - ACT_TILES[j] - DVE_TILES[j]
                pool.tensor_tensor(tiles(h_ring[j % 4])[:, 0:t, :], tiles(g_ring[j])[:, 0:t, :],
                                   spread(f_rs[:, j % 4, 0:t], t, C), ALU.mult).then_inc(f_norm, 1)

            def step(b, p, c, d):
                l1 = exists(b)
                if l1:
                    for w in range(2):
                        pool.wait_ge(s_emb_sg, 2 * b + w + 1)
                        pool.tensor_tensor(emb_f[w][0][:], emb_f[w][0][:], emb_f[w][1][:], ALU.mult).then_inc(s_emb_v, 1)
                    pool.wait_ge(s_msg_pre, b + 1)
                    wait(pool, s_nmp, b)
                    settle(pool, s_passed_pool)
                    pool.tensor_scalar(msg_tok[:], msg_pre[:], 0.0, None, ALU.max).then_inc(s_msg_tok, 1)
                if b is None:
                    rstd(0, d)
                if c is not None:
                    rstd(1, c)
                if b is None and c is not None:
                    vectors()
                if l1:
                    edges(b, p, 0)
                if ends(b, B):
                    slot(0, 4)
                if later(b):
                    rstd(3, b - 1)
                if ends(b, B):
                    slot(0, 5)
                if l1:
                    edges(b, p, 2)
                if c is not None:
                    rstd(2, c)
                if l1:
                    pool.wait_ge(s_x_conv, 2 * b + 2)
                    wait(pool, s_z_ps, b)
                    pool.tensor_tensor(x_conv[1][:], conv_pre[:], x_conv[0][:].bitcast(F32), ALU.subtract).then_inc(s_x_conv_lo, 1)
                if d is not None:
                    if b is not None:
                        rstd(0, d)
                    pool.wait_ge(s_deg, 3 * d + 3)
                    wait(pool, s_x1, d)
                    pool.tensor_tensor(deg0[:, 2, :], deg0[:, 1, :], half_neg[:, 0:NT], ALU.pow).then_inc(s_dinv, 1)
                    pool.wait_ge(s_dinv, 2 * d + 1)
                    pool.tensor_tensor(dinv[:], deg0[:, 2, :], deg0[:, 0, :], ALU.mult).then_inc(s_dinv, 1)

            steps(pool, step)
            slots(pool, slot)

        @block.tensor
        def _(pe):
            pe.wait_ge(s_ident, 1)
            pe.wait_ge(s_folded0, 1)
            for j in range(2):
                m = pe.transpose(bank[CONV][:, C * j:C * j + C], nat[:, N_W0 + j, :], ident[:])
            m.then_inc(s_wturn0, 1)

            def spread_vectors():
                pe.wait_ge(s_folded1, 1)
                pe.matmul(bank[TURN_A][0:KB, 0:C], b1_cols, ident[:], start=True, stop=True)
                for j in range(8):
                    m = pe.matmul(bank[TURN_A][0:KD, 2 * (C + j):2 * (C + j) + 1],
                                  emb_row[:, j, :, :].rearrange("o q i -> o (q i)")[:, 0:KD],
                                  ident[0:1, 0:1], start=True, stop=True)
                m.then_inc(s_rows, 1)

            def turn_weights(first, last):
                for f in range(first, last):
                    wait(pe, s_wlow, f - 3)
                    for i in range(4 if f < FILLS - 1 else 2):
                        k = 4 * f + i
                        rows = P
                        if f == FILLS - 1:
                            src = nat[:, (N_W1, N_MSG)[i], :]
                        elif k < TAPS:
                            src = conv2_nat[:, :, k]
                        elif k < NSPLIT:
                            src = nat[:, k - TAPS + N_IH, :]
                        else:
                            src, rows = nat[0:NSE, N_SE, :], NSE
                        m = pe.transpose(bank[CONV + f % 4][:, C * i:C * i + rows], src, ident[0:rows, 0:rows])
                    m.then_inc(s_wturn, 1)

            def w(j):
                return wt[0][:, j, :], wt[1][:, j, :]

            def product(dst, lhs, rhs, start=True, stop=True):
                pe.matmul(dst, lhs[0], rhs[0], start=start, stop=False)
                pe.matmul(dst, lhs[0], rhs[1], start=False, stop=False)
                return pe.matmul(dst, lhs[1], rhs[0], start=False, stop=stop)

            def cut(parts, first, count):
                return parts[0][:, first:first + count], parts[1][:, first:first + count]

            def turn(k, n):
                pe.wait_ge(s_norm[k], n + 1)
                for t in range(NT):
                    m = pe.transpose(bank[TURN_X][:, P * t:P * t + P], xh[:, t, :], ident[:])
                m.then_inc(s_turn[k], 1)

            def tokens(dst, lhs, weight, done):
                for t in range(NT):
                    m = pe.matmul(dst[:, C * t:C * t + C], lhs[:, P * t:P * t + P], w_full[:, weight, :], start=True, stop=True)
                m.then_inc(done, 1)

            def aggregate(q, first, last):
                for mt in range(first, last):
                    m = pe.matmul(bank[TURN_B], xs[:, mt, :], adj_t[q][:, mt, :], start=(mt == 0), stop=(mt == NT - 1))
                return m

            def adj_turn(d, p, mt):
                if mt >= 2:
                    pe.wait_ge(s_adjt_even if mt == 2 else s_adjt_odd, 2 * d + 1)
                bk = bank[TURN_A if mt % 2 == 0 else TURN_B]
                for t in range(NT):
                    m = pe.transpose(bk[:, P * t:P * t + P], adj_in[p][:, t, P * mt:P * mt + P], ident[:])
                m.then_inc(s_adj_turned, 1)

            def step(b, p, c, d):
                q = 1 - p
                l1 = exists(b)
                l0 = c is not None

                def conv2(first, last):
                    if not l1:
                        return
                    if first == 0:
                        pe.wait_ge(s_h1_lo, b + 1)
                        wait(pe, s_conv_pre, b)
                    for k in range(first, last):
                        m = product(bank[CONV], w(CONV2 + k), cut(h_pad, k, N), start=(k == 0), stop=(k == TAPS - 1))
                    if last == TAPS:
                        m.then_inc(s_conv2, 1)

                def dist(mt):
                    if not l1:
                        return
                    if mt == 0:
                        pe.wait_ge(s_emb_lo, b + 1)
                        wait(pe, s_r, b)
                    if mt == 1:
                        wait(pe, s_z, b)
                    if mt >= 2:
                        pe.wait_ge(s_exp, 4 * b + mt - 1)
                    pe.matmul(bank[DIST_A + mt % 2], emb_m[:, P * mt:P * mt + P], emb_n[:],
                              start=True, stop=True).then_inc(s_dist, 1)

                if l1:
                    if isinstance(b, int) and b == 0:
                        pe.wait_ge(s_ready, 1)
                    pe.wait_ge(s_xt[2], b + 1)
                    pe.wait_ge(s_xl, b + 1)
                    wait(pe, s_x_nmp_lo, b)
                    product(bank[CHAN], w(CONV1), cut(xc_s, 0, N)).then_inc(s_conv1, 1)
                    pe.wait_ge(s_xc, b + 1)
                    pe.wait_ge(s_x2, b + 1)
                    tokens(bank[TOK], xc[p], MSG, s_msg)
                if l0:
                    pe.wait_ge(s_xs, c + 1)
                    pe.wait_ge(s_adjt_even, 2 * c + 2)
                    pe.wait_ge(s_adjt_odd, 2 * c + 2)
                    if b is not None:
                        wait(pe, s_gh_n, b)
                    aggregate(q, 0, 2)
                if l1:
                    pe.wait_ge(s_h1, b + 1)
                    product(bank[CHAN][0:KD, :], [x[:].rearrange("p q i -> p (q i)")[:, 0:KD] for x in wse],
                            cut(xc_s, 0, N)).then_inc(s_emb, 1)
                if l0:
                    aggregate(q, 2, NT).then_inc(s_q, 1)
                conv2(0, 4)
                if l0:
                    if b is None:
                        pe.wait_ge(s_wfull, 1)
                    pe.wait_ge(s_xt[0], c + 1)
                    if l1:
                        pe.wait_ge(s_msg_pre, b + 1)
                    tokens(bank[TOK], xh_t, W0, s_agg)
                    if b is None:
                        spread_vectors()
                        turn_weights(0, 4)
                conv2(4, 7)
                if later(b):
                    pe.wait_ge(s_upd, b)
                    if not l1:
                        pe.wait_ge(s_x3, b - 1)
                    for t in range(NT):
                        m = pe.transpose(bank[TURN_X][:, C * t:C * t + C], upd[:, P * t:P * t + P], ident[:])
                    m.then_inc(s_back, 1)
                dist(0)
                dist(1)
                conv2(7, 15)
                if l0:
                    if later(b):
                        pe.wait_ge(s_x3, b)
                    turn(1, c)
                dist(2)
                dist(3)
                conv2(15, 16)
                if l0:
                    pe.wait_ge(s_xt[1], c + 1)
                    pe.wait_ge(s_agg_scaled, c + 1)
                    tokens(bank[TOK], xh_t, WF, s_ffn)
                    if b is None:
                        turn_weights(4, FILLS)
                conv2(16, TAPS)
                if d is not None:
                    if b is None and l0:
                        pe.wait_ge(s_rows_read, 1)
                    pe.wait_ge(s_in[p], loaded(d, p))
                    if later(b):
                        pe.wait_ge(s_n_pre, b)
                    adj_turn(d, p, 0)
                    adj_turn(d, p, 1)
                if l1:
                    pe.wait_ge(s_msg_tok, b + 1)
                    for mt in range(NT):
                        if mt % 2 == 0:
                            pe.wait_ge(s_edge_p, 2 * b + mt // 2 + 1)
                        else:
                            pe.wait_ge(s_edge_v, 2 * b + mt // 2 + 1)
                        m = pe.matmul(bank[CHAN], msg_tok[:, mt, :], edge[:, mt, :], start=(mt == 0), stop=(mt == NT - 1))
                    m.then_inc(s_nmp, 1)
                if d is not None:
                    adj_turn(d, p, 2)
                    adj_turn(d, p, 3)
                if l1:
                    x_in = cut(xc_s, 0, N)
                    pe.wait_ge(s_exp, 4 * b + 4)
                    product(bank[DIST_A], w(HH), x_in, stop=False)
                    product(bank[DIST_B], w(HH + 1), x_in, stop=False)
                    if d is not None:
                        pe.wait_ge(s_adjt_odd, 2 * d + 2)
                    elif not l0:
                        pe.wait_ge(s_gh_n, b)
                    product(bank[TURN_B], w(HH + 2), x_in).then_inc(s_ghn_ps, 1)
                if l0:
                    turn(2, c)
                if l1:
                    x_c, x_n = cut(x_conv, 0, N), cut(x_nmp, 0, N)
                    pe.wait_ge(s_x_conv, 2 * b + 1)
                    pe.wait_ge(s_x_conv_lo, b + 1)
                    product(bank[DIST_A], w(IH), x_c, start=False, stop=False)
                    product(bank[DIST_B], w(IH + 2), x_c, start=False, stop=False)
                    pe.wait_ge(s_x_nmp, b + 1)
                    pe.wait_ge(s_x_nmp_lo, b + 1)
                    product(bank[DIST_A], w(IH + 1), x_n, start=False).then_inc(s_r_ps, 1)
                    if d is not None:
                        pe.wait_ge(s_adjt_even, 2 * d + 2)
                    else:
                        pe.wait_ge(s_n_pre, b)
                    product(bank[TURN_A], w(IH + 4), x_c, stop=False)
                    product(bank[TURN_A], w(IH + 5), x_n, start=False).then_inc(s_gin_ps, 1)
                if l1:
                    product(bank[DIST_B], w(IH + 3), x_n, start=False).then_inc(s_z_ps, 1)

            steps(pe, step)

            def slot(it, k):
                before = earlier(it, k, LAG_T)
                if before is not None:
                    i, j, s = before
                    pe.wait_ge(f_norm, s + 1)
                    pe.wait_ge(f_norm_act, s + 1)
                    if DVE_TILES[j]:
                        pe.wait_ge(f_norm_dve, dve_norms(i, j) + 1)
                    wait(pe, f_state, s - 1)
                    for t in range(GT):
                        m = pe.transpose(g_ps[j % 2][:, t // NT, P * (t % NT):P * (t % NT) + P],
                                         tiles(h_ring[j % 4])[:, t, :], ident[:])
                    m.then_inc(f_turn, 1)
                if not (isinstance(it, int) and it == 0):
                    s = (it - 1) * GROUPS + k
                    pe.wait_ge(f_state, s + 1)
                    if isinstance(it, int) and it == ITERS:
                        if k >= 2:
                            pe.wait_ge(f_out, k - 1)
                        else:
                            pe.wait_ge(f_u, ITERS * GROUPS - 1 + k)
                    else:
                        pe.wait_ge(f_u, s + GROUPS - 1)
                    for h in range(2):
                        pe.matmul(y_ps[k % 2][:, h, :], ones_bf[:], bias1[:].rearrange("p t c -> p (t c)"),
                                  start=True, stop=False, skip_group_check=True)
                        for t in range(NT):
                            m = pe.matmul(y_ps[k % 2][:, h, C * t:C * t + C], y_all[:, GT * k + NT * h + t, :], w1_t[:],
                                          start=False, stop=True, skip_group_check=True)
                    m.then_inc(f_mm, 1)

            slots(pe, slot)


        @block.scalar
        def _(act):
            act.wait_ge(s_wturn0, 1)
            act.activation(w_full[:, W0:W0 + 2, :], tiles(bank[CONV])[:, 0:2, :], ACT.Copy).then_inc(s_wfull, 1)

            def vec(c):
                return bcol[:, c:c + 1]

            def weights_high(first, last):
                for f in range(first, last):
                    act.wait_ge(s_wturn, f + 1)
                    n = min(4, NSPLIT - 4 * f)
                    ins = act.activation(wt[0][:, 4 * f:4 * f + n, :], tiles(bank[CONV + f % 4])[:, 0:n, :], ACT.Copy)
                    if f == FILLS - 2:
                        ins = act.activation(parts_se(0), embedding(), ACT.Copy)
                    ins.then_inc(s_whigh, 1)
                if last < FILLS - 1:
                    return
                act.wait_ge(s_wturn, FILLS)
                act.activation(w1_t[:], bank[CONV + (FILLS - 1) % 4][:, 0:C], ACT.Copy)
                act.activation(w_full[:, MSG, :], bank[CONV + (FILLS - 1) % 4][:, C:2 * C], ACT.Copy).then_inc(s_whigh, 1)
                act.wait_ge(s_vectors, 1)

            def adjt_even(c, q, mt):
                act.wait_ge(s_adj_turned, 4 * c + mt + 1)
                wait(act, s_edge_p, 2 * (c - 1))
                wait(act, s_edge_v, 2 * (c - 1))
                act.activation(adj_t[q][:, mt, :], bank[TURN_A], ACT.Copy).then_inc(s_adjt_even, 1)

            def exp(b, mt):
                act.wait_ge(s_dist, 4 * b + mt + 1)
                wait(act, s_nmp, b)
                act.activation(edge[:, mt, :], bank[DIST_A + mt % 2], ACT.Exp).then_inc(s_exp, 1)

            def slot(it, k):
                before = earlier(it, k, LAG_S)
                if before is not None:
                    _, j, s = before
                    act.wait_ge(f_u, s + 1)
                    act.activation(g_ring[j], u_ring[j % 2], ACT.Silu).then_inc(f_silu, 1)
                before = earlier(it, k, LAG_T)
                if before is not None:
                    _, j, s = before
                    act.wait_ge(f_turn, s + 1)
                    act.activation(y_all[:, GT * j:GT * j + GT, :].rearrange("p t c -> p (t c)"),
                                   g_ps[j % 2].rearrange("p h n -> p (h n)"), ACT.Copy).then_inc(f_state, 1)
                if not (isinstance(it, int) and it == ITERS):
                    if isinstance(it, int) and it == 0:
                        act.wait_ge(s_norm[3], GT // NT * (k + 1))
                        src = y_all[:, GT * k:GT * k + GT, :].rearrange("p t c -> p (t c)")
                    else:
                        act.wait_ge(f_mm, (it - 1) * GROUPS + k + 1)
                        src = y_ps[k % 2].rearrange("p h n -> p (h n)")
                    wait(act, f_u, it * GROUPS + k - 1)
                    act.activation(t_ring[k % 2], src, ACT.Tanh).then_inc(f_tanh, 1)
                before = earlier(it, k, LAG_A)
                if before is not None:
                    _, j, s = before
                    act.wait_ge(f_pow, s + 1)
                    wait(act, f_turn, s - 3)
                    for t in range(GT - ACT_TILES[j], GT):
                        ins = act.activation(tiles(h_ring[j % 4])[:, t, :], tiles(g_ring[j])[:, t, :], ACT.Copy,
                                             scale=f_rs[:, j % 4, t:t + 1])
                    ins.then_inc(f_norm_act, 1)

            def step(b, p, c, d):
                q = 1 - p
                l1 = exists(b)
                l0 = c is not None
                if l1:
                    act.wait_ge(s_conv1, b + 1)
                    wait(act, s_conv2, b)
                    act.activation(h_full[:], bank[CHAN], ACT.Relu, bias=vec(SH1), scale=vec(SC1))
                    act.activation(h_pad[0][:, HALO:HALO + N], bank[CHAN], ACT.Relu, bias=vec(SH1), scale=vec(SC1)).then_inc(s_h1, 1)
                    act.wait_ge(s_emb, b + 1)
                    wait(act, s_emb_lo, b)
                    for m in range(2):
                        for k in range(2):
                            j = 4 * m + 2 * k
                            ins = act.activation(emb_f[m][k][:], bank[CHAN][0:KD, :], ACT.Identity,
                                                 bias=emb_vec[:, j + 1:j + 2], scale=emb_vec[:, j:j + 1])
                        ins.then_inc(s_emb_sg, 1)
                if later(b):
                    act.wait_ge(s_n_pre, b)
                    wait(act, s_upd, b - 1)
                    act.activation(n_act[:], n_pre, ACT.Tanh, bias=vec(BN_)).then_inc(s_n, 1)
                if l0:
                    act.wait_ge(s_q, c + 1)
                    wait(act, s_ffn, c)
                    act.activation(xh_t[:], bank[TURN_B], ACT.Copy).then_inc(s_xt[0], 1)
                if ends(b, B):
                    slot(0, 4)
                    slot(0, 5)
                if l1:
                    wait(act, s_dist, 4 * b)
                    for m, emb in enumerate((emb_m, emb_n)):
                        act.wait_ge(s_emb_v, 2 * b + m + 1)
                        act.activation(emb[:], emb_f[m][0][:], ACT.Copy).then_inc(s_emb_hi, 1)
                    exp(b, 0)
                    exp(b, 1)
                if l0:
                    if b is None:
                        weights_high(0, 4)
                    act.wait_ge(s_turn[1], c + 1)
                    act.wait_ge(s_agg, c + 1)
                    act.activation(xh_t[:], bank[TURN_X], ACT.Copy, bias=1.0).then_inc(s_xt[1], 1)
                    if b is None:
                        weights_high(4, FILLS - 1)
                if l1:
                    exp(b, 2)
                    exp(b, 3)
                if ends(b, B - 1):
                    slot(0, 0)
                    slot(0, 1)
                if d is not None:
                    adjt_even(d, p, 0)
                if l1:
                    act.wait_ge(s_conv_pre, b + 1)
                    wait(act, s_z_ps, b)
                    act.activation(x_conv[0][:], conv_pre[:], ACT.Relu, bias=vec(SH2)).then_inc(s_x_conv, 1)
                    act.wait_ge(s_x_conv, 2 * b + 1)
                    act.activation(conv_pre[:], conv_pre[:], ACT.Relu, bias=vec(SH2)).then_inc(s_x_conv, 1)
                if ends(b, B - 1):
                    slot(0, 2)
                if l1:
                    act.wait_ge(s_nmp, b + 1)
                    act.activation(x_nmp[0][:], bank[CHAN], ACT.Copy).then_inc(s_x_nmp, 1)
                if d is not None:
                    adjt_even(d, p, 2)
                if l1:
                    act.wait_ge(s_ghn_ps, b + 1)
                    wait(act, s_rh, b)
                    act.activation(gh_n, bank[TURN_B], ACT.Identity, bias=vec(HNB), scale=0.5).then_inc(s_gh_n, 1)
                if ends(b, B - 1):
                    slot(0, 3)
                if l0:
                    act.wait_ge(s_turn[2], c + 1)
                    if later(b):
                        act.wait_ge(s_x_less_n, b)
                    act.activation(xc[q][:], bank[TURN_X], ACT.Copy).then_inc(s_xc, 1)
                    act.activation(xc_s[0][:], bank[TURN_X], ACT.Copy).then_inc(s_xt[2], 1)
                if l1:
                    act.wait_ge(s_r_ps, b + 1)
                    act.activation(gate_r, bank[DIST_A], ACT.Tanh, bias=vec(RZB), scale=0.5).then_inc(s_r, 1)
                if l1:
                    act.wait_ge(s_z_ps, b + 1)
                    wait(act, s_z_part, b)
                    act.activation(gate_z, bank[DIST_B], ACT.Tanh, bias=vec(ZZB), scale=0.5).then_inc(s_z, 1)

            steps(act, step)
            slots(act, slot)

        @block.vector
        def _(dve):
            count = [0]

            def link(ins):
                count[0] += 1
                ins.then_inc(s_fold, 1)
                dve.wait_ge(s_fold, count[0])

            def vec(c):
                return bcol[:, c:c + 1]

            dve.memset(half_neg[:], -0.5)
            dve.memset(ident[:], 1.0).then_inc(s_const, 1)
            dve.memset(ones_bf[:], 1.0)
            dve.memset(bias1[:], 0.0)
            dve.memset(b1_cols, 0.0)
            for k in range(2):
                dve.memset(wse[k][:].bitcast(F32), 0.0)
                dve.memset(h_pad[k][:].bitcast(F32), 0.0)
            link(dve.memset(emb_row, 0.0))
            for j, t, value in EMB_CONST:
                ins = dve.memset(emb_row[:, j, :, NSE * t:NSE * t + NSE], value)
            link(ins)
            dve.wait_ge(s_first, 16 * 4)
            first = nat[:, N_W0:N_W0 + 2, :]
            link(dve.tensor_reduce(bcol[:, T0:T0 + 2], first, AX_X, ALU.add))
            link(dve.tensor_tensor(bcol[:, U0:U0 + 2], bcol[:, B0:B0 + 2], bcol[:, T0:T0 + 2], ALU.subtract))
            link(dve.tensor_scalar(bcol[:, T0:T0 + 2], bcol[:, U0:U0 + 2], 1.0 / C, None, ALU.mult))
            dve.tensor_tensor(first, first, spread(bcol[:, T0:T0 + 2], 2, C), ALU.add).then_inc(s_folded0, 1)

            def fold():
                w1_nat = nat[:, N_W1, :]
                dve.wait_ge(s_small, 16 * NSMALL)
                dve.wait_ge(s_wload, 16 * NWEIGHTS)
                link(dve.tensor_tensor(tmp_w, w1_nat, lnb_row, ALU.mult))
                dve.tensor_tensor(w1_nat, w1_nat, lnw_row, ALU.mult)
                link(dve.tensor_reduce(vec(FB1), tmp_w, AX_X, ALU.add))
                link(dve.tensor_reduce(vec(B0), w1_nat, AX_X, ALU.add))
                dve.tensor_tensor(vec(FB1), vec(FB1), vec(B1), ALU.add)
                link(dve.tensor_scalar(vec(BF), vec(B0), -1.0 / C, None, ALU.mult))
                dve.tensor_scalar(w1_nat, w1_nat, vec(BF), float(C) ** 0.5, ALU.add, ALU.mult)
                for r in range(3):
                    dve.tensor_copy(b1_cols[:, 32 * r:32 * r + 1], vec(FB1))
                for j, t, scale in EMB_BIAS:
                    ins = dve.tensor_scalar(emb_row[:, j, :, NSE * t:NSE * t + NSE],
                                            emb_bias.rearrange("o (q i) -> o q i", q=1).broadcast_to([1, 4, NSE]),
                                            scale, None, ALU.mult)
                ins.then_inc(s_folded1, 1)

            def weights_low(first, last):
                for f in range(first, last):
                    dve.wait_ge(s_whigh, f + 1)
                    n = min(4, NSPLIT - 4 * f)
                    ins = dve.tensor_tensor(wt[1][:, 4 * f:4 * f + n, :], tiles(bank[CONV + f % 4])[:, 0:n, :],
                                            wt[0][:, 4 * f:4 * f + n, :].bitcast(F32), ALU.subtract)
                    if f == FILLS - 2:
                        ins = dve.tensor_tensor(parts_se(1), embedding(), parts_se(0).bitcast(F32), ALU.subtract)
                    ins.then_inc(s_wlow, 1)

            def take_rows():
                dve.wait_ge(s_rows, 1)
                dve.tensor_copy(emb_vec[:], bank[TURN_A][0:KD, 2 * C:2 * C + 16].rearrange("p (j o) -> p j o", o=2)[:, :, 0])
                dve.tensor_copy(part_f[:, 0, :], bank[TURN_A][0:KB, 0:C]).then_inc(s_rows_read, 1)

            def split_bias():
                dve.wait_ge(s_whigh, FILLS)
                dve.wait_ge(s_wlow, FILLS - 1)
                dve.wait_ge(s_vectors, 1)
                dve.wait_ge(s_rows_read, 1)
                dve.sem_inc(s_ready, 1)
                link(dve.tensor_copy(part_bf[:, 0, :], part_f[:, 0, :]))
                link(dve.tensor_tensor(part_f[:, 1, :], part_f[:, 0, :], part_bf[:, 0, :], ALU.subtract))
                link(dve.tensor_copy(part_bf[:, 1, :], part_f[:, 1, :]))
                link(dve.tensor_tensor(part_f[:, 2, :], part_f[:, 1, :], part_bf[:, 1, :], ALU.subtract))
                link(dve.tensor_copy(part_bf[:, 2, :], part_f[:, 2, :]))
                for t in range(NT):
                    for r in range(3):
                        dve.tensor_copy(bias1[32 * r:32 * r + 1, t, :], part_bf[32 * r:32 * r + 1, r, :])

            def x_graph(b):
                return x_tok[:, graph(b), :]

            def stats(w, n):
                settle(dve, s_passed_dve)
                for t in range(NT):
                    ins = dve.bn_stats(ln_stat[:, w, t, :], x_tok[:, bass.ds(n * NT + t, 1), :].rearrange("p t c -> p (t c)"))
                ins.then_inc(s_stat[w], 1)
                dve.wait_ge(s_stat[w], n + 1)
                settle(dve, s_passed_dve)
                for t in range(NT):
                    ins = dve.bn_aggr(ln_mv[:, w, t, :], ln_stat[:, w, t, :])
                ins.then_inc(s_mv[w], 1)

            def degree(d, p):
                dve.wait_ge(s_in[p], loaded(d, p))
                wait(dve, s_dinv, 2 * d)
                dve.tensor_reduce(deg[:], adj_in[p], AX_X, ALU.add).then_inc(s_deg, 1)
                dve.wait_ge(s_deg, 3 * d + 1)
                dve.tensor_scalar(deg0[:, 0, :], deg[:], 0.0, None, ALU.not_equal).then_inc(s_deg, 1)
                dve.scalar_tensor_tensor(out=deg0[:, 1, :], in0=deg[:], scalar=0.0, in1=deg[:],
                                         op0=ALU.is_equal, op1=ALU.add).then_inc(s_deg, 1)

            def norm(w, n):
                dve.wait_ge(s_rs[w], 2 * n + 2)
                if w == 0:
                    wait(dve, s_turn[2], n)
                elif w == 1:
                    dve.wait_ge(s_xs, n + 1)
                elif w == 2:
                    dve.wait_ge(s_turn[1], n + 1)
                for t in range(NT):
                    dst = xh[:, t:t + 1, :] if w < 3 else y_all[:, bass.ds(n * NT + t, 1), :]
                    ins = dve.tensor_scalar(dst, x_tok[:, bass.ds(n * NT + t, 1), :], ln_mv[:, w, t, 0:1],
                                            ln_rs[:, w, t:t + 1], ALU.subtract, ALU.mult)
                ins.then_inc(s_norm[w], 1)

            def adjt_odd(c, q, mt):
                dve.wait_ge(s_adj_turned, 4 * c + mt + 1)
                wait(dve, s_edge_p, 2 * (c - 1))
                dve.tensor_copy(adj_t[q][:, mt, :], bank[TURN_B]).then_inc(s_adjt_odd, 1)

            def edges(b, p, mt):
                dve.wait_ge(s_exp, 4 * b + mt + 1)
                dve.tensor_tensor(edge[:, mt, :], edge[:, mt, :], adj_t[p][:, mt, :], ALU.mult).then_inc(s_edge_v, 1)

            def slot(it, k):
                before = earlier(it, k, LAG_A)
                if before is not None and DVE_TILES[before[1]]:
                    _, j, s = before
                    dve.wait_ge(f_pow, s + 1)
                    wait(dve, f_turn, s - 3)
                    first = GT - ACT_TILES[j] - DVE_TILES[j]
                    for t in range(first, first + DVE_TILES[j]):
                        ins = dve.tensor_scalar(tiles(h_ring[j % 4])[:, t, :], tiles(g_ring[j])[:, t, :],
                                                f_rs[:, j % 4, t:t + 1], None, ALU.mult)
                    ins.then_inc(f_norm_dve, 1)
                group = slice(GT * k, GT * k + GT)
                if isinstance(it, int) and it == ITERS:
                    dve.wait_ge(f_mm, (ITERS - 1) * GROUPS + k + 1)
                    dve.tensor_tensor(y_all[:, group, :], x_tok[:, group, :],
                                      y_ps[k % 2].rearrange("p h (t c) -> p (h t) c", c=C), ALU.add).then_inc(f_out, 1)
                else:
                    s = it * GROUPS + k
                    dve.wait_ge(f_tanh, s + 1)
                    wait(dve, f_silu, s - 1)
                    if isinstance(it, int) and it == 0:
                        src = y_all[:, group, :].rearrange("p t c -> p (t c)")
                    else:
                        src = y_ps[k % 2].rearrange("p h n -> p (h n)")
                    dve.scalar_tensor_tensor(out=u_ring[k % 2], in0=t_ring[k % 2], scalar=STEP, in1=src,
                                             op0=ALU.mult, op1=ALU.add).then_inc(f_u, 1)
                now, before = earlier(it, k, LAG_S), earlier(it, k, LAG_V)

                def bn(first, last):
                    if now is None:
                        return
                    _, j, s = now
                    if first == 0:
                        dve.wait_ge(f_silu, s + 1)
                        wait(dve, f_sm, s * 2 - 2)
                    for t in range(first, last):
                        ins = dve.bn_stats(f_stat[:, j % 2, t, :], g_ring[j][:, C * t:C * t + C])
                    if last == GT:
                        ins.then_inc(f_bn, 1)

                bn(0, 2)
                if before is not None:
                    _, j, s = before
                    r = j % 2
                    dve.wait_ge(f_bn, s + 1)
                    dve.tensor_tensor(f_small[:, 0, :], f_stat[:, r, :, 1], f_stat[:, r, :, 4], ALU.subtract)
                    dve.scalar_tensor_tensor(out=f_small[:, 1, :], in0=f_stat[:, r, :, 2], scalar=C * EPS,
                                             in1=f_stat[:, r, :, 5], op0=ALU.add, op1=ALU.add).then_inc(f_sm, 1)
                bn(2, 4)
                if before is not None:
                    dve.wait_ge(f_sm, s * 2 + 1)
                    dve.scalar_tensor_tensor(out=f_small[:, 2, :], in0=f_small[:, 0, :], scalar=C / 4,
                                             in1=f_small[:, 0, :], op0=ALU.mult, op1=ALU.mult).then_inc(f_sm, 1)
                bn(4, 6)
                if before is not None:
                    dve.wait_ge(f_sm, s * 2 + 2)
                    wait(dve, f_pow, s - 1)
                    dve.tensor_tensor(f_var[:, r, :], f_small[:, 1, :], f_small[:, 2, :], ALU.add).then_inc(f_v, 1)
                bn(6, GT)

            def step(b, p, c, d):
                q = 1 - p
                l1 = exists(b)
                l0 = c is not None
                if l0:
                    dve.wait_ge(s_norm[0], c + 1)
                    dve.wait_ge(s_dinv, 2 * c + 2)
                    wait(dve, s_q, c)
                    dve.scalar_tensor_tensor(out=xs[:], in0=xh[:], scalar=1.0, in1=spread(dinv[:], NT, C),
                                             op0=ALU.add, op1=ALU.mult).then_inc(s_xs, 1)
                    if b is None:
                        fold()
                        degree(d, p)
                        stats(0, d)
                if d is not None and (b is not None or not l0):
                    degree(d, p)
                    if b is None:
                        stats(0, d)
                if l1:
                    dve.wait_ge(s_h1, b + 1)
                    wait(dve, s_conv2, b)
                    dve.tensor_tensor(h_pad[1][:, HALO:HALO + N], h_full[:], h_pad[0][:, HALO:HALO + N].bitcast(F32),
                                      ALU.subtract).then_inc(s_h1_lo, 1)
                if l1:
                    dve.wait_ge(s_msg, b + 1)
                    wait(dve, s_msg_tok, b)
                    dve.tensor_tensor(msg_pre[:], tiles(bank[TOK]),
                                      bmsg_row[:].rearrange("p (o c) -> p o c", o=1).broadcast_to([P, NT, C]),
                                      ALU.add).then_inc(s_msg_pre, 1)
                if later(b):
                    dve.wait_ge(s_r, b)
                    dve.wait_ge(s_gh_n, b)
                    wait(dve, s_n, b - 1)
                    dve.scalar_tensor_tensor(out=n_pre, in0=gate_r, scalar=1.0, in1=gh_n,
                                             op0=ALU.add, op1=ALU.mult).then_inc(s_rh, 1)
                    dve.wait_ge(s_rh, b)
                    dve.wait_ge(s_gin_ps, b)
                    dve.tensor_tensor(n_pre, n_pre, bank[TURN_A], ALU.add).then_inc(s_n_pre, 1)
                    dve.wait_ge(s_n, b)
                    dve.tensor_tensor(x_less_n[:], xc[q][:], n_act[:], ALU.subtract).then_inc(s_x_less_n, 1)
                    dve.wait_ge(s_x_less_n, b)
                    dve.wait_ge(s_z, b)
                    dve.scalar_tensor_tensor(out=x_less_n[:], in0=gate_z, scalar=1.0, in1=x_less_n[:],
                                             op0=ALU.add, op1=ALU.mult).then_inc(s_z_part, 1)
                    dve.wait_ge(s_z_part, b)
                    wait(dve, s_back, b - 1)
                    dve.scalar_tensor_tensor(out=upd[:], in0=x_less_n[:], scalar=0.5, in1=n_act[:],
                                             op0=ALU.mult, op1=ALU.add).then_inc(s_upd, 1)
                if ends(b, B):
                    slot(0, 4)
                if l1:
                    dve.wait_ge(s_emb_hi, 2 * b + 2)
                    for m, emb, first, last in ((0, emb_m, 2, 4), (1, emb_n, 1, 2), (1, emb_n, 3, 4)):
                        rows = slice(QUAD * first, min(QUAD * last, KD))
                        ins = dve.tensor_tensor(emb[rows, :], emb_f[m][0][rows, :], emb[rows, :].bitcast(F32), ALU.subtract)
                    ins.then_inc(s_emb_lo, 1)
                if l0:
                    dve.wait_ge(s_agg, c + 1)
                    dve.tensor_tensor(agg_tok[:], tiles(bank[TOK]), spread(dinv[:], NT, C), ALU.mult).then_inc(s_agg_scaled, 1)
                    dve.wait_ge(s_agg_scaled, c + 1)
                    dve.scalar_tensor_tensor(out=x_graph(c), in0=agg_tok[:], scalar=0.0, in1=x_graph(c),
                                             op0=ALU.max, op1=ALU.add).then_inc(s_x1, 1)
                    dve.wait_ge(s_x1, c + 1)
                    stats(1, c)
                if later(b):
                    dve.wait_ge(s_back, b)
                    dve.tensor_tensor(x_graph(b - 1), x_graph(b - 1), tiles(bank[TURN_X]), ALU.add).then_inc(s_x3, 1)
                if l0:
                    norm(1, c)
                    if b is None:
                        weights_low(0, 4)
                        take_rows()
                if l1:
                    edges(b, p, 1)
                if later(b):
                    dve.wait_ge(s_x3, b)
                    stats(3, b - 1)
                if ends(b, B):
                    slot(0, 5)
                if l1:
                    edges(b, p, 3)
                if later(b):
                    norm(3, b - 1)
                if ends(b, B - 1):
                    slot(0, 0)
                    slot(0, 1)
                if l0:
                    dve.wait_ge(s_ffn, c + 1)
                    dve.tensor_tensor(x_graph(c), x_graph(c), tiles(bank[TOK]), ALU.add).then_inc(s_x2, 1)
                    dve.wait_ge(s_x2, c + 1)
                    stats(2, c)
                if l1:
                    dve.wait_ge(s_conv2, b + 1)
                    wait(dve, s_x_conv_lo, b)
                    dve.scalar_tensor_tensor(out=conv_pre[:], in0=bank[CONV], scalar=vec(SC2), in1=xc[p][:],
                                             op0=ALU.mult, op1=ALU.add).then_inc(s_conv_pre, 1)
                if ends(b, B - 1):
                    slot(0, 2)
                if d is not None:
                    adjt_odd(d, p, 1)
                if l0:
                    if b is None:
                        weights_low(4, 6)
                    norm(2, c)
                    if b is None:
                        weights_low(6, 7)
                if d is not None:
                    adjt_odd(d, p, 3)
                    if b is not None:
                        stats(0, d)
                if l1:
                    dve.wait_ge(s_x_nmp, b + 1)
                    wait(dve, s_z_ps, b)
                    dve.tensor_tensor(x_nmp[1][:], bank[CHAN], x_nmp[0][:].bitcast(F32), ALU.subtract).then_inc(s_x_nmp_lo, 1)
                if ends(b, B - 1):
                    slot(0, 3)
                if l0:
                    dve.wait_ge(s_xt[2], c + 1)
                    dve.tensor_tensor(xc_s[1][:], xc[q][:], xc_s[0][:].bitcast(F32), ALU.subtract).then_inc(s_xl, 1)
                if d is not None:
                    norm(0, d)
                    if b is None and l0:
                        split_bias()

            steps(dve, step)
            slots(dve, slot)


_INS = ['x', 'adj', 'L0_gnn_W', 'L0_gnn_b', 'L0_ffn_weight', 'L0_ffn_bias', 'L1_gnn_w_se', 'L1_gnn_b_se',
        'L1_gnn_conv1_w', 'L1_gnn_bn1_g', 'L1_gnn_bn1_b', 'L1_gnn_bn1_m', 'L1_gnn_bn1_v', 'L1_gnn_conv2_w',
        'L1_gnn_bn2_g', 'L1_gnn_bn2_b', 'L1_gnn_bn2_m', 'L1_gnn_bn2_v', 'L1_gnn_w_msg', 'L1_gnn_b_msg',
        'L1_gnn_w_ih', 'L1_gnn_b_ih', 'L1_gnn_w_hh', 'L1_gnn_b_hh', 'L1_ffn_ln_w', 'L1_ffn_ln_b', 'L1_ffn_W',
        'L1_ffn_b']


def kernel(**inputs):
    import numpy as _np
    import concourse.bacc as _bacc
    from concourse import mybir as _mybir
    from concourse.bass_utils import run_bass_kernel_spmd as _run

    nc = _bacc.Bacc("TRN2", target_bir_lowering=False, num_devices=1)
    arrays, aps = {}, {}
    for name in _INS:
        a = _np.ascontiguousarray(inputs[name])
        arrays[f"in_{name}_dram"] = a
        aps[name] = nc.dram_tensor(f"in_{name}_dram", a.shape, _mybir.dt.from_np(a.dtype), kind="ExternalInput").ap()
    out = nc.dram_tensor("out_0_dram", inputs['x'].shape, _mybir.dt.float32, kind="ExternalOutput").ap()
    g = {k[len('L1_gnn_'):]: v for k, v in aps.items() if k.startswith('L1_gnn_')}
    build(nc, aps['x'], aps['adj'], aps['L0_gnn_W'], aps['L0_gnn_b'], aps['L0_ffn_weight'], aps['L0_ffn_bias'],
          g['w_se'], g['b_se'], g['conv1_w'], [g['bn1_g'], g['bn1_b'], g['bn1_m'], g['bn1_v']],
          g['conv2_w'], [g['bn2_g'], g['bn2_b'], g['bn2_m'], g['bn2_v']], g['w_msg'], g['b_msg'],
          g['w_ih'], g['b_ih'], g['w_hh'], g['b_hh'], aps['L1_ffn_ln_w'], aps['L1_ffn_ln_b'],
          aps['L1_ffn_W'], aps['L1_ffn_b'], out)
    r = _run(nc, [arrays], core_ids=[0])
    return r.results[0]["out_0_dram"]
```
